# Optimizing a Trainium2 kernel written in Bass

```python
import numpy as np
import jax
import jax.numpy as jnp

def _softmax(x, axis=-1):
    return jax.nn.softmax(x, axis=axis)

def _gelu(x):
    return jax.nn.gelu(x, approximate=True)

def _silu(x):
    return jax.nn.silu(x)

def _sigmoid(x):
    return jax.nn.sigmoid(x)

def _layernorm(x, axis=-1, eps=1e-05):
    m = jnp.mean(x, axis=axis, keepdims=True)
    v = jnp.var(x, axis=axis, keepdims=True)
    return (x - m) / jnp.sqrt(v + eps)

def _scatter_add(tgt, idx, src, axis=0):
    return tgt.at[idx].add(src)

def _segment_sum(src, seg, n):
    return jax.ops.segment_sum(src, seg, n)
kernel_name = 'mk_seq_preln_d1_jaxref_r8_173942'

def setup_inputs(seed: int=0):
    np.random.seed(seed)
    _w = jnp.asarray

    def _L0_attn_setup():
        import jax, jax.numpy as jnp
        import numpy as np
        B, S, D = (2, 256, 512)
        H = 32
        HD = D // H
        THETA = 10000.0

        def _rope_cos_sin(seq_len, head_dim, theta=THETA):
            inv = 1.0 / theta ** (np.arange(0, head_dim, 2)[:head_dim // 2].astype(np.float32) / head_dim)
            t = np.arange(seq_len)
            f = np.outer(t, inv).astype(np.float32)
            return (jnp.asarray(np.cos(f)), jnp.asarray(np.sin(f)))

        def _apply_rotary(x, cos, sin):
            xr = x.astype(jnp.float32).reshape(*x.shape[:-1], HD // 2, 2)
            x0, x1 = (xr[..., 0], xr[..., 1])
            c = cos[None, :, None, :]
            s = sin[None, :, None, :]
            o0 = x0 * c - x1 * s
            o1 = x0 * s + x1 * c
            return jnp.stack((o0, o1), axis=-1).reshape(*x.shape[:-1], HD)
        key = jax.random.key(seed)
        ks = jax.random.split(key, 5)
        std = 0.02
        return {'x': jax.random.normal(ks[0], (B, S, D), dtype=jnp.float32), 'wq': jax.random.normal(ks[1], (D, D), dtype=jnp.float32) * std, 'wk': jax.random.normal(ks[2], (D, D), dtype=jnp.float32) * std, 'wv': jax.random.normal(ks[3], (D, D), dtype=jnp.float32) * std, 'wo': jax.random.normal(ks[4], (D, D), dtype=jnp.float32) * std}
    _L0_attn_in = _L0_attn_setup()

    def _L0_ffn_setup():
        import jax, jax.numpy as jnp
        import numpy as np
        D_IN = 512
        D_OUT = 512
        RANK = 16
        NUM_EXPERTS = 8
        TOP_K = 2
        SCALING = 32.0 / RANK
        key = jax.random.key(seed)
        ks = jax.random.split(key, 6)
        x = jax.random.normal(ks[0], (4, 256, D_IN), dtype=jnp.float32)
        W_base = jax.random.normal(ks[1], (D_OUT, D_IN), dtype=jnp.float32) * (1.0 / np.sqrt(D_IN))
        b_base = jax.random.normal(ks[2], (D_OUT,), dtype=jnp.float32) * 0.01
        W_router = jax.random.normal(ks[3], (NUM_EXPERTS, D_IN), dtype=jnp.float32) * 0.01
        A_stack = jax.random.uniform(ks[4], (NUM_EXPERTS, RANK, D_IN), dtype=jnp.float32, minval=-1.0, maxval=1.0) * (1.0 / np.sqrt(D_IN))
        B_stack = jax.random.normal(ks[5], (NUM_EXPERTS, D_OUT, RANK), dtype=jnp.float32) * 0.02
        return {'x': x, 'W_base': W_base, 'b_base': b_base, 'W_router': W_router, 'A_stack': A_stack, 'B_stack': B_stack}
    _L0_ffn_in = _L0_ffn_setup()
    _d = {'L0_attn_x': _L0_attn_in['x'], 'L0_attn_wq': _L0_attn_in['wq'], 'L0_attn_wk': _L0_attn_in['wk'], 'L0_attn_wv': _L0_attn_in['wv'], 'L0_attn_wo': _L0_attn_in['wo'], 'L0_ffn_W_base': _L0_ffn_in['W_base'], 'L0_ffn_b_base': _L0_ffn_in['b_base'], 'L0_ffn_W_router': _L0_ffn_in['W_router'], 'L0_ffn_A_stack': _L0_ffn_in['A_stack'], 'L0_ffn_B_stack': _L0_ffn_in['B_stack']}
    _x0 = _d['L0_attn_x']
    _d['L0_attn_x'] = jax.random.normal(jax.random.fold_in(jax.random.key(seed), 1), (2, 1024, 512), dtype=_x0.dtype)
    del _x0
    return _d

def reference(L0_attn_x, L0_attn_wq, L0_attn_wk, L0_attn_wv, L0_attn_wo, L0_ffn_W_base, L0_ffn_b_base, L0_ffn_W_router, L0_ffn_A_stack, L0_ffn_B_stack):

    def _L0_attn_ref(x, wq, wk, wv, wo):
        import jax, jax.numpy as jnp
        import numpy as np
        B, S, D = (2, 256, 512)
        H = 32
        HD = D // H
        THETA = 10000.0

        def _rope_cos_sin(seq_len, head_dim, theta=THETA):
            inv = 1.0 / theta ** (np.arange(0, head_dim, 2)[:head_dim // 2].astype(np.float32) / head_dim)
            t = np.arange(seq_len)
            f = np.outer(t, inv).astype(np.float32)
            return (jnp.asarray(np.cos(f)), jnp.asarray(np.sin(f)))

        def _apply_rotary(x, cos, sin):
            xr = x.astype(jnp.float32).reshape(*x.shape[:-1], HD // 2, 2)
            x0, x1 = (xr[..., 0], xr[..., 1])
            c = cos[None, :, None, :]
            s = sin[None, :, None, :]
            o0 = x0 * c - x1 * s
            o1 = x0 * s + x1 * c
            return jnp.stack((o0, o1), axis=-1).reshape(*x.shape[:-1], HD)
        b, s, d = x.shape
        q = (x @ wq).reshape(b, s, H, HD)
        k = (x @ wk).reshape(b, s, H, HD)
        v = (x @ wv).reshape(b, s, H, HD)
        cos, sin = _rope_cos_sin(s, HD)
        q = _apply_rotary(q, cos, sin)
        k = _apply_rotary(k, cos, sin)
        scale = 1.0 / jnp.sqrt(jnp.float32(HD))
        scores = jnp.einsum('bqhd,bkhd->bhqk', q, k) * scale
        causal = jnp.tril(jnp.ones((s, s), dtype=bool))
        scores = jnp.where(causal[None, None], scores, jnp.finfo(scores.dtype).min)
        probs = jax.nn.softmax(scores, axis=-1)
        out = jnp.einsum('bhqk,bkhd->bqhd', probs, v).reshape(b, s, d)
        return out @ wo

    def _L0_ffn_ref(x, W_base, b_base, W_router, A_stack, B_stack):
        import jax, jax.numpy as jnp
        import numpy as np
        D_IN = 512
        D_OUT = 512
        RANK = 16
        NUM_EXPERTS = 8
        TOP_K = 2
        SCALING = 32.0 / RANK
        orig_shape = x.shape
        xf = x.reshape(-1, D_IN)
        logits = xf @ W_router.T
        probs = jax.nn.softmax(logits, axis=-1)
        topk_p, topk_i = jax.lax.top_k(probs, TOP_K)
        topk_p = topk_p / jnp.sum(topk_p, axis=-1, keepdims=True)
        combine = jnp.sum(jax.nn.one_hot(topk_i, NUM_EXPERTS, dtype=xf.dtype) * topk_p[..., None], axis=1)
        h = jnp.einsum('nd,erd->ner', xf, A_stack)
        h = h * combine[..., None]
        lora_out = jnp.einsum('ner,eor->no', h, B_stack) * SCALING
        base_out = xf @ W_base.T + b_base
        out = base_out + lora_out
        return out.reshape(orig_shape[:-1] + (D_OUT,))
    x = L0_attn_x
    x = x + _L0_attn_ref(_layernorm(x, axis=-1), L0_attn_wq, L0_attn_wk, L0_attn_wv, L0_attn_wo)
    x = x + _L0_ffn_ref(_layernorm(x, axis=-1), L0_ffn_W_base, L0_ffn_b_base, L0_ffn_W_router, L0_ffn_A_stack, L0_ffn_B_stack)
    return x

_drawn_inputs = setup_inputs


def setup_inputs(seed=0):
    import zlib

    import numpy as np

    out = dict(_drawn_inputs(seed))
    spreads = {}
    factors = {'L0_attn_wq': 8.0,
     'L0_attn_wk': 8.0,
     'L0_attn_wv': 3.314,
     'L0_attn_wo': 3.211,
     'L0_ffn_b_base': 8.0}
    for name, (base, spread) in spreads.items():
        noise = np.random.default_rng([zlib.crc32(name.encode()), seed]).standard_normal(out[name].shape)
        drawn = base * np.exp(spread * noise) if base else spread * noise
        out[name] = jnp.asarray(drawn.astype(out[name].dtype))
    for name, factor in factors.items():
        out[name] = (out[name] * factor).astype(out[name].dtype)
    return out
```

```python
from contextlib import ExitStack

import numpy as np

import concourse.bass as bass
from concourse import mybir

F32 = mybir.dt.float32
BF16 = mybir.dt.bfloat16
U32 = mybir.dt.uint32
ACT = mybir.ActivationFunctionType
ALU = mybir.AluOpType
AX = mybir.AxisListType

P = 128
B, S, D = 2, 1024, 512
H, HD = 32, 16
E, R = 8, 16
ER = E * R
KT = D // P
CHUNK = 512
CHUNKS = S // CHUNK
TPC = CHUNK // P
NCH = B * CHUNKS
QH = 4
NG = H // QH
ROUNDS = B * NG
GW = QH * HD
TT = S // P
PARTS = 3
SLOTS = 6
KROWS = SLOTS * HD
MROWS = KROWS + 2
THETA = 10000.0
EPS = 1e-5
SCALE = float(HD) ** -0.5
LORA_SCALE = 32.0 / R
MASKED = -1e30
LOWEST = -3e38
RING = 3
G3 = 4
TRIPS3 = B * TT // G3
STAGED = 16 * (5 + KT)


def max_tasks():
    tasks = []
    for i in range(TT):
        width = (i + 1) * P
        for part, w in enumerate([min(width, CHUNK)] + ([width - CHUNK] if width > CHUNK else [])):
            per = min(QH, CHUNK // w)
            per = 1 if per == 3 else per
            for h in range(0, QH, per):
                tasks.append((i, part, h, per, w))
    return tasks


def preln_block(nc, x, wq, wk, wv, wo, w_base, b_base, w_router, a_stack, b_stack, cos_t, sin_t, consts, out):
    tasks = max_tasks()
    NT = len(tasks)
    units = [(1, j) for j in range(TT)] + [(0, j) for j in range(TPC)]
    NU = len(units)
    assert NU % RING == 0 and NT % 2 == 0 and ROUNDS % RING == 1
    last_of = {1: TT - 1, 0: TPC - 1}
    work = [512 - max(0, j - 4 * c) * P for c, j in units]
    share, given = [], 0
    for u in range(NU):
        upto = NT if u >= NU - 2 else min(NT, round(NT * sum(work[:u + 1]) / sum(work[:NU - 2])))
        share.append((given, upto))
        given = upto
    NORM_AT = TT + 1

    with ExitStack() as ctx:
        def sb(name, shape, dt=F32):
            return ctx.enter_context(nc.sbuf_tensor(name, shape, dt))

        def sem(name):
            return ctx.enter_context(nc.semaphore(name))

        v_all = sb("v_all", [P, TT, ROUNDS * GW])
        att = sb("att", [P, TT, ROUNDS * GW])
        cst = sb("cst", [P, 3 * P + E])
        ident_b = sb("ident_b", [P, P], BF16)
        mask_q = sb("mask_q", [P, P], BF16)
        mask_k = sb("mask_k", [P, P], BF16)
        wo_sb = sb("wo_sb", [P, KT, D])
        wbT = sb("wbT", [P, KT, D])
        arT = sb("arT", [P, KT, ER + E])
        bT = sb("bT", [P, D])
        bias = sb("bias", [P, D])
        small = sb("small", [P, 280])
        mxp = sb("mxp", [P, QH, TT, 2])
        nm = sb("nm", [P, QH * TT])
        mrow = sb("mrow", [P, 2, P], BF16)
        rc = sb("rc", [P, TPC, QH])
        ident = cst[:, 0:P]
        iota = cst[:, 3 * P:3 * P + E]
        KB = 256
        arena = sb("arena", [P, 94 * KB])

        def region(at, n):
            return arena[:, int(at * KB):int((at + n) * KB)]

        wqkv = region(0, 24).rearrange("p (w k n) -> p w k n", w=3, k=KT)
        xin = region(24, 16).rearrange("p (c t d) -> p c t d", c=2, t=TPC)
        xT = region(40, 16).rearrange("p (c k n) -> p c k n", c=2, k=KT)
        cs = region(56, 8).rearrange("p (w n) -> p w n", w=2)
        qf, t1, sw, t2, ro, r1 = (region(64 + 4 * k, 4).rearrange("p (s n) -> p s n", s=2) for k in range(6))
        pc = region(88, 6).bitcast(BF16).rearrange("p (s a n) -> p s a n", s=2, a=PARTS)

        qs = region(0, 24).bitcast(BF16).rearrange("p (s h n) -> p s h n", s=RING, h=QH)
        ks = region(24, 24).bitcast(BF16).rearrange("p (s h n) -> p s h n", s=RING, h=QH)
        pr = region(48, 24).rearrange("p (s h n) -> p s h n", s=RING, h=QH)
        vs = region(72, 12).rearrange("p (s j h d) -> p s j h d", s=RING, j=TT, h=QH)
        ot = region(84, 4).rearrange("p (c n) -> p c n", c=2)

        xr = region(0, 32).rearrange("p (j b d) -> p j b d", j=TT, b=B)
        at3, x1, xn, y3 = (region(32 + 8 * k, 8).rearrange("p (u n) -> p u n", u=G3) for k in range(4))
        attT, xnT = (region(64 + 4 * k, 4).rearrange("p (u k n) -> p u k n", u=2, k=KT) for k in range(2))
        h3 = region(72, 2).rearrange("p (u n) -> p u n", u=G3)
        hT = region(74, 1).rearrange("p (u n) -> p u n", u=2)
        attf = att[:].rearrange("p t n -> p (t n)")
        wb_st = attf[:, 0:KT * D].rearrange("p (o n) -> p o n", o=KT)
        a_st = attf[:, 2048:2560]
        b_st = attf[:, 2560:3072].rearrange("p (o e r) -> p o e r", o=KT, e=E)
        r_st = attf[0:E, 3072:3584]

        ps = ctx.enter_context(nc.psum_tensor("ps", [P, 8, 512], F32))
        pieces = nc.dram_tensor("pieces", [2, PARTS, ROUNDS, QH, HD, S], BF16).ap()

        stats = small[:, 0:24].rearrange("p (t n) -> p t n", t=4)
        mv = small[:, 24:32].rearrange("p (t n) -> p t n", t=4)
        veps = small[:, 32:36]
        rstd = small[:, 36:40]
        mhalf = small[:, 40:44]
        top = small[:, 48:80].rearrange("p (u n) -> p u n", u=4)
        topi = small[:, 80:112].bitcast(U32).rearrange("p (u n) -> p u n", u=4)
        idxf = small[:, 112:120].rearrange("p (u n) -> p u n", u=4)
        gap = small[:, 120:124]
        ex = small[:, 124:128]
        den = small[:, 128:132]
        w0 = small[:, 132:136]
        w1 = small[:, 136:140]
        comb0 = small[:, 144:176].rearrange("p (u n) -> p u n", u=4)
        comb = small[:, 176:208].rearrange("p (u n) -> p u n", u=4)
        lg = small[:, 208:240].rearrange("p (u n) -> p u n", u=4)
        comb1 = small[:, 240:272].rearrange("p (u n) -> p u n", u=4)

        consts_loaded, weights_loaded, staged = sem("consts_loaded"), sem("weights_loaded"), sem("staged")
        tables_loaded = sem("tables_loaded")
        x_loaded = [sem(f"x_loaded{c}") for c in range(2)]
        consts_ready, half_ready = sem("consts_ready"), sem("half_ready")
        aggr_done, rstd_ready, xn_ready = sem("aggr_done"), sem("rstd_ready"), sem("xn_ready")
        carried = sem("carried")
        stats_done, eps_added = sem("stats_done"), sem("eps_added")
        m1_ready, rc_ready = sem("m1_ready"), sem("rc_ready")
        dve_step = sem("dve_step")
        tp_ready, xT_ready = sem("tp_ready"), sem("xT_ready")
        qk_ready, qf_ready = sem("qk_ready"), sem("qf_ready")
        v_ready, v_copied = sem("v_ready"), sem("v_copied")
        t1_ready, ro_ready, p1_ready, r1_ready, p2_ready, p3_ready = (
            sem(n) for n in ("t1_ready", "ro_ready", "p1_ready", "r1_ready", "p2_ready", "p3_ready"))
        stored = [sem(f"stored{s}") for s in range(2)]
        wt_ready, wt_copied = sem("wt_ready"), sem("wt_copied")
        ones_set, vs_ready = sem("ones_set"), sem("vs_ready")
        stack_loaded = [sem(f"stack_loaded{s}") for s in range(RING)]
        rows_ready, rows_loaded = sem("rows_ready"), sem("rows_loaded")
        q_scores, q_reduced = sem("q_scores"), sem("q_reduced")
        nm_ready, mt_ready, misc_free = sem("nm_ready"), sem("mt_ready"), sem("misc_free")
        k_scores, exp_done, pv_done = sem("k_scores"), sem("exp_done"), sem("pv_done")
        o_copied, ot_ready = sem("o_copied"), sem("ot_ready")
        xr_loaded, at_ready = sem("xr_loaded"), sem("at_ready")
        tr_ready, tr_copied = sem("tr_ready"), sem("tr_copied")
        mm_ready, mm_read = sem("mm_ready"), sem("mm_read")
        x1_ready, aggr3, eps3, rstd3, xn3 = (sem(n) for n in ("x1_ready", "aggr3", "eps3", "rstd3", "xn3"))
        x1b_ready, gap_ready, ex_ready, h_ready = (sem(n) for n in ("x1b_ready", "gap_ready", "ex_ready", "h_ready"))
        y_psum, y_read, y_stored = sem("y_psum"), sem("y_read"), sem("y_stored")

        TP, QK, VP = (0, 1), (2, 3, 4, 5), (6, 7)
        KS_BANK, QS_BANK, O_BANK, MISC = 0, 4, 6, 7
        BASE, TR, MM = 0, 4, 6

        def alone(eng):
            eng.sem_inc(carried, 1)

        block = ctx.enter_context(nc.Block())
        xrows = x.rearrange("b (c t p) d -> (b c) p t d", c=CHUNKS, p=P)

        @block.sync
        def _(sp):
            for done in (*stored, y_stored):
                sp.sem_inc(done, 16)
            sp.dma_start(cst[:], consts).then_inc(consts_loaded, 16)
            sp.dma_start(xin[:, 0], xrows[0]).then_inc(x_loaded[0], 16)
            for w, src in enumerate((wq, wk, wv)):
                sp.dma_start(wqkv[:, w], src.rearrange("(k p) n -> p k n", p=P)).then_inc(weights_loaded, 16)
            sp.dma_start(cs[:, 0], cos_t).then_inc(tables_loaded, 16)
            sp.dma_start(cs[:, 1], sin_t).then_inc(tables_loaded, 16)
            sp.dma_start(xin[:, 1], xrows[1]).then_inc(x_loaded[1], 16)
            sp.dma_start(wo_sb[:], wo.rearrange("(k p) n -> p k n", p=P)).then_inc(staged, 16)
            sp.dma_start(wb_st, w_base.rearrange("(o p) n -> p o n", p=P)).then_inc(staged, 16)
            sp.dma_start(a_st, a_stack.rearrange("e r n -> (e r) n")).then_inc(staged, 16)
            sp.dma_start(r_st, w_router).then_inc(staged, 16)
            for o in range(KT):
                sp.dma_start(b_st[:, o], b_stack[:, o * P:(o + 1) * P, :].rearrange("e p r -> p e r")).then_inc(staged, 16)
            sp.dma_start(bias[:], b_base.partition_broadcast(P)).then_inc(staged, 16)

            for k in range(NCH):
                b, c = k // CHUNKS, k % CHUNKS
                for m in range(2 * KT):
                    t = 2 * KT * k + m
                    sp.wait_ge(p3_ready, 2 + t + 1)
                    dst = pieces[m // KT].rearrange("a n h d t -> (n h d) a t")
                    row = b * NG * GW + (m % KT) * P
                    sp.dma_start(dst[row:row + P, :, c * CHUNK:(c + 1) * CHUNK], pc[:, t % 2]).then_inc(stored[t % 2], 16)
                    if m == 0 and k + 1 < NCH and k >= 1:
                        sp.wait_ge(tp_ready, TPC * k)
                        sp.dma_start(xin[:, (k + 1) % 2], xrows[k + 1]).then_inc(x_loaded[(k + 1) % 2], 16)

            for s in range(2):
                sp.wait_ge(stored[s], 16 * (1 + NCH * KT))
            sp.wait_ge(v_copied, 2 + TPC * NCH)

            def load_round(n, s):
                for qk, dst, use in ((0, qs, (0, 0, 0, 1, 1, 2)), (1, ks, (0, 1, 2, 0, 1, 0))):
                    for slot, part in enumerate(use):
                        src = pieces[qk, part].rearrange("n h d t -> d n h t")[:, bass.ds(n, 1)]
                        sp.dma_start(dst[HD * slot:HD * (slot + 1), s], src.rearrange("d n h t -> d (n h) t")).then_inc(
                            stack_loaded[s], 16)

            def load_rows(n, s):
                sp.wait_ge(rows_ready, n + 1)
                for a in range(2):
                    sp.dma_start(qs[KROWS + a:KROWS + a + 1, s].rearrange("p h (i t) -> p (h i) t", t=P), mrow[0:QH * TT, a, :]).then_inc(
                        rows_loaded, 16)

            for n in range(RING):
                load_round(n, n)
            load_rows(0, 0)
            with sp.Fori(0, (ROUNDS - 1) // RING - 1) as i:
                for u in range(RING):
                    n = i * RING + u
                    load_rows(n + 1, (u + 1) % RING)
                    sp.wait_ge(pv_done, RING + NU * (n + 1))
                    load_round(n + RING, u)
            for n in range(ROUNDS - 1 - RING, ROUNDS - 1):
                load_rows(n + 1, (n + 1) % RING)
                if n + RING < ROUNDS:
                    sp.wait_ge(pv_done, RING + NU * (n + 1))
                    load_round(n + RING, n % RING)

            sp.wait_ge(misc_free, 1 + 3 * ROUNDS)
            for b in range(B):
                sp.dma_start(xr[:, :, b], x[b].rearrange("(j p) d -> p j d", p=P)).then_inc(xr_loaded, 16)
            with sp.Fori(0, TRIPS3) as i:
                for u in range(G3):
                    sp.wait_ge(y_read, G3 + i * G3 + u + 1)
                    dst = out[u % B].rearrange("(j p) d -> p j d", p=P)[:, bass.ds(i * (G3 // B) + u // B, 1)]
                    sp.dma_start(dst.rearrange("p j d -> p (j d)"), y3[:, u]).then_inc(y_stored, 16)
            sp.wait_ge(y_stored, 16 + 16 * B * TT)

        @block.gpsimd
        def _(pool):
            nc.gpsimd.memset(mhalf, -0.5).then_inc(half_ready, 1)
            pool.sem_inc(p3_ready, 2)
            pool.wait_ge(tables_loaded, 32)
            pool.wait_ge(half_ready, 1)
            with pool.Fori(0, B) as b:
                for c in range(CHUNKS):
                    k = b * CHUNKS + c
                    pool.wait_ge(aggr_done, k + 1)
                    alone(pool)
                    nc.gpsimd.tensor_scalar(veps, mv[:, :, 1], EPS, 1.0, ALU.add, ALU.mult).then_inc(eps_added, 1)
                    pool.wait_ge(eps_added, k + 1)
                    nc.gpsimd.tensor_tensor(rstd, veps, mhalf, ALU.pow).then_inc(rstd_ready, 1)
                    for m in range(2 * KT + 1):
                        t = k * 2 * KT + m
                        if m < 2 * KT:
                            pool.wait_ge(qf_ready, t + 1)
                            nc.gpsimd.tensor_tensor(t1[:, m % 2], qf[:, m % 2], cs[:, 0, c * CHUNK:(c + 1) * CHUNK],
                                                    ALU.mult).then_inc(t1_ready, 1)
                        if m >= 1:
                            pool.wait_ge(p2_ready, t)
                            v = (m - 1) % 2
                            nc.gpsimd.tensor_tensor(pc[:, v, 2], r1[:, v], pc[:, v, 1], ALU.subtract).then_inc(p3_ready, 1)

            pool.wait_ge(v_copied, 2 + TPC * NCH)
            for s in range(2):
                pool.wait_ge(stored[s], 16 * (1 + NCH * KT))
            nc.gpsimd.memset(ks[KROWS:MROWS], 1.0).then_inc(ones_set, 1)
            pool.wait_ge(ones_set, 1)
            nc.gpsimd.memset(vs[:, :, :, :, HD:2 * HD], 1.0).then_inc(ones_set, 1)

            def gather_v(n, s):
                src = v_all[:, :, bass.ds(n * GW, GW)].rearrange("p j (h d) -> p j h d", h=QH)
                nc.gpsimd.tensor_copy(vs[:, s, :, :, 0:HD], src).then_inc(vs_ready, 1)

            for n in range(RING):
                gather_v(n, n)
            with pool.Fori(0, (ROUNDS - 1) // RING - 1) as i:
                for u in range(RING):
                    n = i * RING + u
                    pool.wait_ge(pv_done, RING + NU * (n + 1))
                    gather_v(n + RING, u)
            pool.wait_ge(pv_done, RING + NU * (ROUNDS - RING))
            gather_v(ROUNDS - 1, (ROUNDS - 1) % RING)

            pool.wait_ge(misc_free, 1 + 3 * ROUNDS)
            with pool.Fori(0, TRIPS3) as i:
                for u in range(G3):
                    t = i * G3 + u
                    if u == 0:
                        pool.wait_ge(x1b_ready, i + 1)
                    nc.gpsimd.tensor_copy(at3[:, u], attf[:, bass.ds(i * (G3 * D) + u * D, D)]).then_inc(at_ready, 1)
                for u in range(G3):
                    t = i * G3 + u
                    pool.wait_ge(aggr3, t + 1)
                    alone(pool)
                    nc.gpsimd.tensor_scalar(veps[:, u:u + 1], mv[:, u, 1:2], EPS, 1.0, ALU.add, ALU.mult).then_inc(eps3, 1)
                    pool.wait_ge(eps3, t + 1)
                    nc.gpsimd.tensor_tensor(rstd[:, u:u + 1], veps[:, u:u + 1], mhalf[:, 0:1], ALU.pow).then_inc(rstd3, 1)

        @block.scalar
        def _(act):
            act.sem_inc(v_copied, 2)
            with act.Fori(0, B) as b:
                for c in range(CHUNKS):
                    k = b * CHUNKS + c
                    for t in range(TPC):
                        act.wait_ge(tp_ready, k * TPC + t + 1)
                        nc.scalar.copy(xT[:, c, :, t * P:(t + 1) * P], ps[:, TP[t % 2]].rearrange("p (k n) -> p k n", k=KT)).then_inc(
                            xT_ready, 1)
                    for m in range(2 * KT + 2):
                        t = k * 2 * KT + m
                        if m < 2 * KT:
                            act.wait_ge(qk_ready, t + 1)
                            nc.scalar.copy(qf[:, m % 2], ps[:, QK[m % 4]]).then_inc(qf_ready, 1)
                        if 1 <= m <= 2 * KT:
                            v = (m - 1) % 2
                            act.wait_ge(ro_ready, t)
                            act.wait_ge(stored[v], 16 + 16 * (k * KT + (m - 1) // 2))
                            nc.scalar.copy(pc[:, v, 0], ro[:, v]).then_inc(p1_ready, 1)
                        if m >= 2:
                            act.wait_ge(r1_ready, t - 1)
                            nc.scalar.copy(pc[:, m % 2, 1], r1[:, m % 2]).then_inc(p2_ready, 1)
                    for t in range(TPC):
                        act.wait_ge(v_ready, k * TPC + t + 1)
                        nc.scalar.copy(v_all[:, c * TPC + t, bass.ds(b * D, D)], ps[:, VP[t % 2]]).then_inc(v_copied, 1)

            def exps(n, u, slot):
                c, j = units[u]
                w = CHUNK - max(0, j - c * TPC) * P
                for hp in range(2):
                    act.wait_ge(k_scores, 2 * NU * n + 2 * u + hp + 1)
                    if hp == 0:
                        act.wait_ge(pv_done, NU * n + u + 1)
                    nc.scalar.activation(pr[:, slot, 2 * hp:2 * hp + 2, 0:w], ps[:, KS_BANK + 2 * hp:KS_BANK + 2 * hp + 2, 0:w],
                                         ACT.Exp, scale=SCALE).then_inc(exp_done, 1)

            def copy_output(n, cc, done):
                act.wait_ge(pv_done, RING + NU * n + done)
                act.wait_ge(ot_ready, 2 * n + cc + 1)
                nc.scalar.copy(ot[:, cc], ps[:, O_BANK]).then_inc(o_copied, 1)

            def act_round(n):
                for u in range(NU):
                    exps(n, u, u % RING)
                    if u == TT:
                        copy_output(n, 0, TT)
                copy_output(n, 1, NU)

            act.sem_inc(exp_done, 2)
            act.sem_inc(o_copied, 1)
            with act.Fori(0, (ROUNDS - 1) // RING) as i:
                for u in range(RING):
                    act_round(i * RING + u)
            act_round(ROUNDS - 1)

            act.wait_ge(misc_free, 1 + 3 * ROUNDS)
            act.sem_inc(tr_copied, 2)
            with act.Fori(0, TRIPS3) as i:
                def copy_tr(y, dst, shape=None):
                    act.wait_ge(tr_ready, i * 3 * G3 + y + 1)
                    src = ps[:, TR + y % 2]
                    src = src.rearrange("p (k n) -> p k n", k=KT) if shape is None else src[:, 0:shape]
                    nc.scalar.copy(dst, src).then_inc(tr_copied, 1)

                def router_exp(u):
                    act.wait_ge(gap_ready, i * G3 + u + 1)
                    nc.scalar.activation(ex[:, u:u + 1], gap[:, u:u + 1], ACT.Exp).then_inc(ex_ready, 1)

                for u in range(G3):
                    copy_tr(u, attT[:, u % 2])
                for u in range(G3):
                    copy_tr(G3 + u, xnT[:, u % 2])
                    if u >= 1:
                        router_exp(u - 1)
                router_exp(G3 - 1)
                for u in range(G3):
                    copy_tr(2 * G3 + u, hT[:, u % 2], P)

        @block.vector
        def _(dve):
            steps = [0]

            def link(ins, base):
                steps[0] += 1
                ins.then_inc(dve_step, 1)
                dve.wait_ge(dve_step, base + steps[0])

            dve.wait_ge(consts_loaded, 16)
            nc.vector.tensor_copy(ident_b[:], ident)
            nc.vector.tensor_copy(mask_q[:], cst[:, P:2 * P])
            nc.vector.tensor_copy(mask_k[:], cst[:, 2 * P:3 * P])
            nc.vector.memset(mxp[:], LOWEST).then_inc(consts_ready, 1)
            dve.wait_ge(tables_loaded, 32)
            swap = [l ^ 1 for l in range(32)]
            per1 = 2 * (2 * KT)
            with dve.Fori(0, B) as b:
                for c in range(CHUNKS):
                    k = b * CHUNKS + c
                    dve.wait_ge(x_loaded[c], 16 * (b + 1))
                    for t in range(TPC):
                        nc.vector.bn_stats(stats[:, t], xin[:, c, t]).then_inc(stats_done, 1)
                    for t in range(TPC):
                        dve.wait_ge(stats_done, k * TPC + t + 1)
                        alone(dve)
                        last = nc.vector.bn_aggr(mv[:, t], stats[:, t])
                    last.then_inc(aggr_done, 1)
                    dve.wait_ge(rstd_ready, k + 1)
                    for t in range(TPC):
                        nc.vector.tensor_scalar(xin[:, c, t], xin[:, c, t], mv[:, t, 0:1], rstd[:, t:t + 1],
                                                ALU.subtract, ALU.mult).then_inc(xn_ready, 1)
                    for m in range(2 * KT + 1):
                        t = k * 2 * KT + m
                        s = m % 2
                        if m < 2 * KT:
                            dve.wait_ge(qf_ready, t + 1)
                            alone(dve)
                            link(nc.vector.stream_shuffle(sw[:, s], qf[:, s], swap), b * CHUNKS * per1)
                            link(nc.vector.tensor_tensor(t2[:, s], sw[:, s], cs[:, 1, c * CHUNK:(c + 1) * CHUNK], ALU.mult),
                                 b * CHUNKS * per1)
                            dve.wait_ge(t1_ready, t + 1)
                            nc.vector.tensor_tensor(ro[:, s], t1[:, s], t2[:, s], ALU.add).then_inc(ro_ready, 1)
                        if m >= 1:
                            v = (m - 1) % 2
                            dve.wait_ge(p1_ready, t)
                            dve.wait_ge(p3_ready, t)
                            nc.vector.tensor_tensor(r1[:, v], ro[:, v], pc[:, v, 0], ALU.subtract).then_inc(r1_ready, 1)
            assert steps[0] == CHUNKS * per1
            steps[0] = 0
            base2 = NCH * per1

            for g, dst in enumerate([wbT[:, k] for k in range(KT)] + [arT[:, :, 0:ER], arT[:, :, ER:ER + E], bT[:]]):
                dve.wait_ge(wt_ready, g + 1)
                src = ps[:, TP[g % 2]]
                if g == KT:
                    src = src.rearrange("p (k n) -> p k n", k=KT)
                if g == KT + 1:
                    src = src[:, 0:KT * E].rearrange("p (k n) -> p k n", k=KT)
                nc.vector.tensor_copy(dst, src).then_inc(wt_copied, 1)

            dve.sem_inc(q_reduced, 2)
            dve.sem_inc(misc_free, 1)

            def maxima(n, first, upto):
                for k in range(first, upto):
                    i, part, h, per, w = tasks[k]
                    dve.wait_ge(q_scores, NT * n + k + 1)
                    src = ps[:, QS_BANK + k % 2, 0:per * w].rearrange("p (h n) -> p h n", h=per)
                    nc.vector.tensor_reduce(mxp[:, h:h + per, i, part], src, AX.X, ALU.max).then_inc(q_reduced, 1)

            def negated_maxima(n, first=False):
                dve.wait_ge(q_reduced, 2 + NT * (n + 1))
                nc.vector.tensor_reduce(nm[:], mxp[:].rearrange("p h i a -> p (h i) a"), AX.X, ALU.max,
                                        negate=True).then_inc(nm_ready, 1)
                dve.wait_ge(mt_ready, n + 1)
                if not first:
                    dve.wait_ge(rows_loaded, 32 * n)
                rows = ps[0:QH * TT, MISC, 0:P]
                nc.vector.tensor_copy(mrow[0:QH * TT, 0], rows).then_inc(m1_ready, 1)
                dve.wait_ge(m1_ready, n + 1)
                nc.vector.tensor_tensor(mrow[0:QH * TT, 1], rows, mrow[0:QH * TT, 0], ALU.subtract).then_inc(rows_ready, 1)
                dve.wait_ge(rows_ready, n + 1)
                dve.sem_inc(misc_free, 1)

            def normalise(n, cc):
                c = units[0][0] if cc == 0 else units[-1][0]
                dve.wait_ge(ot_ready, 2 + 2 * n + cc + 1)
                o = ps[:, MISC].rearrange("p (t h d) -> p t h d", t=TPC, h=QH)
                nc.vector.reciprocal(rc[:], o[:, :, :, HD]).then_inc(rc_ready, 1)
                dve.wait_ge(rc_ready, 2 * n + cc + 1)
                dst = att[:, c * TPC:(c + 1) * TPC, bass.ds(n * GW, GW)].rearrange("p t (h d) -> p t h d", h=QH)
                nc.vector.tensor_tensor(dst, o[:, :, :, 0:HD], rc[:].unsqueeze(3).broadcast_to([P, TPC, QH, HD]),
                                        ALU.mult).then_inc(misc_free, 1)

            def dve_round(n, following=True):
                for u in range(NU):
                    if following:
                        maxima(n + 1, *share[u])
                    if u == NORM_AT:
                        normalise(n, 0)
                if following:
                    negated_maxima(n + 1)
                normalise(n, 1)

            maxima(0, 0, NT)
            negated_maxima(0, True)
            with dve.Fori(0, (ROUNDS - 1) // RING) as i:
                for u in range(RING):
                    dve_round(i * RING + u)
            dve_round(ROUNDS - 1, False)

            dve.sem_inc(mm_read, 2)
            dve.sem_inc(y_read, G3)
            dve.sem_inc(x1b_ready, 1)
            dve.wait_ge(xr_loaded, 16 * B)
            dve.wait_ge(staged, STAGED)
            xrf = xr[:].rearrange("p j b d -> p (j b d)")

            def normal(i, u):
                dve.wait_ge(rstd3, i * G3 + u + 1)
                nc.vector.tensor_scalar(xn[:, u], x1[:, u], mv[:, u, 0:1], rstd[:, u:u + 1],
                                        ALU.subtract, ALU.mult).then_inc(xn3, 1)

            per3 = 11 * G3
            with dve.Fori(0, TRIPS3) as i:
                base = i * per3 + base2
                for u in range(G3):
                    dve.wait_ge(y_read, G3 + i * G3)
                    dve.wait_ge(mm_ready, i * 2 * G3 + u + 1)
                    nc.vector.tensor_tensor(x1[:, u], ps[:, MM + u % 2], xrf[:, bass.ds(i * (G3 * D) + u * D, D)],
                                            ALU.add).then_inc(mm_read, 1)
                    dve.wait_ge(mm_read, i * 2 * G3 + 2 + u + 1)
                    link(nc.vector.bn_stats(stats[:, u], x1[:, u]), base)
                    alone(dve)
                    nc.vector.bn_aggr(mv[:, u], stats[:, u]).then_inc(aggr3, 1)
                    if u >= 1:
                        normal(i, u - 1)
                normal(i, G3 - 1)
                for u in range(G3):
                    last = nc.vector.tensor_tensor(x1[:, u], x1[:, u], bias[:], ALU.add)
                last.then_inc(x1b_ready, 1)
                for u in range(G3):
                    dve.wait_ge(mm_ready, i * 2 * G3 + G3 + u + 1)
                    bank = ps[:, MM + u % 2]
                    link(nc.vector.tensor_copy(lg[:, u], bank[:, ER:ER + E]), base)
                    alone(dve)
                    link(nc.vector.max(top[:, u], lg[:, u]), base)
                    nc.vector.tensor_tensor(gap[:, u:u + 1], top[:, u, 1:2], top[:, u, 0:1], ALU.subtract).then_inc(gap_ready, 1)
                    link(nc.vector.max_index(topi[:, u], top[:, u], lg[:, u]), base)
                    link(nc.vector.tensor_copy(idxf[:, u], topi[:, u, 0:2]), base)
                    dve.wait_ge(ex_ready, i * G3 + u + 1)
                    link(nc.vector.tensor_scalar(den[:, u:u + 1], ex[:, u:u + 1], 1.0, 1.0 / LORA_SCALE, ALU.add, ALU.mult), base)
                    link(nc.vector.reciprocal(w0[:, u:u + 1], den[:, u:u + 1]), base)
                    link(nc.vector.tensor_tensor(w1[:, u:u + 1], w0[:, u:u + 1], ex[:, u:u + 1], ALU.mult), base)
                    link(nc.vector.tensor_scalar(comb0[:, u], iota, idxf[:, u, 0:1], w0[:, u:u + 1], ALU.is_equal, ALU.mult), base)
                    link(nc.vector.tensor_scalar(comb1[:, u], iota, idxf[:, u, 1:2], w1[:, u:u + 1], ALU.is_equal, ALU.mult), base)
                    link(nc.vector.tensor_tensor(comb[:, u], comb0[:, u], comb1[:, u], ALU.add), base)
                    nc.vector.tensor_tensor(h3[:, u].rearrange("p (e r) -> p e r", e=E),
                                            bank[:, 0:ER].rearrange("p (e r) -> p e r", e=E),
                                            comb[:, u].unsqueeze(2).broadcast_to([P, E, R]), ALU.mult).then_inc(mm_read, 1)
                dve.wait_ge(y_stored, 16 + i * (16 * G3))
                dve.wait_ge(x1b_ready, i + 2)
                for u in range(G3):
                    dve.wait_ge(y_psum, i * G3 + u + 1)
                    nc.vector.tensor_tensor(y3[:, u], ps[:, BASE + u], x1[:, u], ALU.add).then_inc(y_read, 1)
            assert steps[0] == per3, steps

        @block.tensor
        def _(pe):
            mm, tr = nc.tensor.matmul, nc.tensor.transpose
            pe.wait_ge(consts_loaded, 16)
            pe.wait_ge(weights_loaded, 48)
            with pe.Fori(0, B) as b:
                for c in range(CHUNKS):
                    k = b * CHUNKS + c
                    for t in range(TPC):
                        pe.wait_ge(xn_ready, k * TPC + t + 1)
                        if t >= 2:
                            pe.wait_ge(xT_ready, k * TPC + t - 1)
                        for kt in range(KT):
                            last = tr(ps[:, TP[t % 2], kt * P:(kt + 1) * P], xin[:, c, t, kt * P:(kt + 1) * P], ident)
                        last.then_inc(tp_ready, 1)
                    pe.wait_ge(xT_ready, k * TPC + TPC)
                    for m in range(2 * KT):
                        if m >= 4:
                            pe.wait_ge(qf_ready, k * 2 * KT + m - 3)
                        for kt in range(KT):
                            last = mm(ps[:, QK[m % 4]], wqkv[:, m // KT, kt, (m % KT) * P:(m % KT + 1) * P], xT[:, c, kt],
                                      start=kt == 0, stop=kt == KT - 1)
                        last.then_inc(qk_ready, 1)
                    for t in range(TPC):
                        pe.wait_ge(v_copied, k * TPC + t + 1)
                        for kt in range(KT):
                            last = mm(ps[:, VP[t % 2]], xT[:, c, kt, t * P:(t + 1) * P], wqkv[:, 2, kt],
                                      start=kt == 0, stop=kt == KT - 1)
                        last.then_inc(v_ready, 1)
                    pe.wait_ge(qf_ready, k * 2 * KT + 2 * KT)

            pe.wait_ge(staged, STAGED)
            for g in range(KT + 3):
                if g >= 2:
                    pe.wait_ge(wt_copied, g - 1)
                bank = ps[:, TP[g % 2]]
                for o in range(KT):
                    if g < KT:
                        last = tr(bank[:, o * P:(o + 1) * P], wb_st[:, o, g * P:(g + 1) * P], ident)
                    elif g == KT:
                        last = tr(bank[:, o * P:(o + 1) * P], a_st[:, o * P:(o + 1) * P], ident)
                    elif g == KT + 1:
                        last = tr(bank[:, o * E:(o + 1) * E], r_st[:, o * P:(o + 1) * P], cst[0:E, 0:E])
                    else:
                        last = tr(bank[:, o * P:(o + 1) * P], b_st[:, o].rearrange("p e r -> p (e r)"), ident)
                last.then_inc(wt_ready, 1)
            pe.wait_ge(wt_copied, KT + 3)
            pe.wait_ge(v_copied, 2 + NCH * TPC)

            pe.wait_ge(consts_ready, 1)
            pe.wait_ge(ones_set, 2)

            def fill_maxima(n, s, first, upto):
                for k in range(first, upto):
                    i, part, h0, per, w = tasks[k]
                    pe.wait_ge(q_reduced, NT * n + k + 1)
                    diagonal = part * CHUNK + w == (i + 1) * P
                    for e in range(per):
                        o = ps[:, QS_BANK + k % 2, e * w:(e + 1) * w]
                        last = mm(o, qs[0:KROWS, s, h0 + e, i * P:(i + 1) * P],
                                  ks[0:KROWS, s, h0 + e, part * CHUNK:part * CHUNK + w], start=True, stop=not diagonal)
                        if diagonal:
                            last = mm(o[:, w - P:w], ident_b[:], mask_q[:], start=False, stop=True)
                    last.then_inc(q_scores, 1)

            def transpose_maxima(n, x_misc):
                pe.wait_ge(nm_ready, n + 1)
                pe.wait_ge(misc_free, x_misc + 1)
                tr(ps[0:QH * TT, MISC, 0:P], nm[:], ident).then_inc(mt_ready, 1)

            def transpose_output(n, cc, x_misc):
                pe.wait_ge(o_copied, 2 * n + cc + 2)
                pe.wait_ge(misc_free, x_misc + 1)
                for t in range(TPC):
                    last = tr(ps[:, MISC, t * P:(t + 1) * P], ot[:, cc, t * P:(t + 1) * P], ident)
                last.then_inc(ot_ready, 1)

            def times_v(n, s, u):
                c, j = units[u]
                q0 = max(0, j - c * TPC) * P
                pe.wait_ge(exp_done, 2 + 2 * NU * n + 2 * u + 2)
                if u == 0:
                    pe.wait_ge(vs_ready, n + 1)
                if j == 0:
                    pe.wait_ge(o_copied, 2 * n + (u > 0) + 1)
                for h in range(QH):
                    last = mm(ps[2 * HD * h:2 * HD * (h + 1), O_BANK, q0:CHUNK], vs[:, s, j, h], pr[:, u % RING, h, 0:CHUNK - q0],
                              start=j == 0, stop=j == last_of[c])
                last.then_inc(pv_done, 1)

            def pe_round(n, s, following=True):
                pe.wait_ge(rows_loaded, 32 * n + 32)
                for u, (c, j) in enumerate(units):
                    q0 = max(0, j - c * TPC) * P
                    w = CHUNK - q0
                    for hp in range(2):
                        pe.wait_ge(exp_done, 2 * NU * n + 2 * u + hp + 1)
                        for e in range(2):
                            h = 2 * hp + e
                            o = ps[:, KS_BANK + h, 0:w]
                            diagonal = j >= c * TPC
                            last = mm(o, ks[0:MROWS, s, h, j * P:(j + 1) * P],
                                      qs[0:MROWS, s, h, c * CHUNK + q0:(c + 1) * CHUNK], start=True, stop=not diagonal)
                            if diagonal:
                                last = mm(o[:, 0:P], ident_b[:], mask_k[:], start=False, stop=True)
                        last.then_inc(k_scores, 1)
                    if following:
                        if u == 0:
                            loads = 16 * 2 * SLOTS
                            pe.wait_ge(stack_loaded[(s + 1) % RING],
                                       n // RING * loads + loads * (1 + (s == RING - 1)) if isinstance(n, int)
                                       else (n - s) * (loads // RING) + loads * (1 + (s == RING - 1)))
                        fill_maxima(n + 1, (s + 1) % RING, *share[u])
                    if u >= 1:
                        times_v(n, s, u - 1)
                    if u == NORM_AT:
                        transpose_output(n, 0, 3 * n + 1)
                times_v(n, s, NU - 1)
                if following:
                    transpose_maxima(n + 1, 3 * n + 2)
                transpose_output(n, 1, 3 * n + 2 + following)

            pe.sem_inc(pv_done, RING)
            pe.sem_inc(ot_ready, 2)
            pe.wait_ge(stack_loaded[0], 16 * 2 * SLOTS)
            fill_maxima(0, 0, 0, NT)
            transpose_maxima(0, 0)
            with pe.Fori(0, (ROUNDS - 1) // RING) as i:
                for u in range(RING):
                    pe_round(i * RING + u, u)
            pe_round(ROUNDS - 1, 0, False)

            pe.wait_ge(misc_free, 1 + 3 * ROUNDS)
            with pe.Fori(0, TRIPS3) as i:
                def transposed(y, src):
                    pe.wait_ge(tr_copied, i * 3 * G3 + y + 1)
                    for kt, block_in in enumerate(src):
                        last = tr(ps[:, TR + y % 2, kt * P:(kt + 1) * P], block_in, ident)
                    last.then_inc(tr_ready, 1)

                def blocks(a):
                    return [a[:, kt * P:(kt + 1) * P] for kt in range(KT)]

                def project(u):
                    pe.wait_ge(tr_copied, i * 3 * G3 + 2 + u + 1)
                    pe.wait_ge(mm_read, i * 2 * G3 + u + 1)
                    for kt in range(KT):
                        last = mm(ps[:, MM + u % 2], attT[:, u % 2, kt], wo_sb[:, kt], start=kt == 0, stop=kt == KT - 1)
                    last.then_inc(mm_ready, 1)

                def dense(u):
                    pe.wait_ge(tr_copied, i * 3 * G3 + 2 + G3 + u + 1)
                    pe.wait_ge(mm_read, i * 2 * G3 + G3 + u + 1)
                    for kt in range(KT):
                        last = mm(ps[:, MM + u % 2, 0:ER + E], xnT[:, u % 2, kt], arT[:, kt], start=kt == 0, stop=kt == KT - 1)
                    last.then_inc(mm_ready, 1)
                    pe.wait_ge(y_read, i * G3 + u + 1)
                    for kt in range(KT):
                        mm(ps[:, BASE + u], xnT[:, u % 2, kt], wbT[:, kt], start=kt == 0, stop=False)

                for u in range(G3 + 1):
                    if u < G3:
                        pe.wait_ge(at_ready, i * G3 + u + 1)
                        transposed(u, blocks(at3[:, u]))
                    if u >= 1:
                        project(u - 1)
                for u in range(G3 + 1):
                    if u < G3:
                        pe.wait_ge(xn3, i * G3 + u + 1)
                        transposed(G3 + u, blocks(xn[:, u]))
                    if u >= 1:
                        dense(u - 1)
                for u in range(G3 + 1):
                    if u < G3:
                        pe.wait_ge(mm_read, i * 2 * G3 + 2 + G3 + u + 1)
                        transposed(2 * G3 + u, [h3[:, u]])
                    if u >= 1:
                        v = u - 1
                        pe.wait_ge(tr_copied, i * 3 * G3 + 2 + 2 * G3 + v + 1)
                        mm(ps[:, BASE + v], hT[:, v % 2], bT[:], start=False, stop=True).then_inc(y_psum, 1)


_INS = ['L0_attn_x', 'L0_attn_wq', 'L0_attn_wk', 'L0_attn_wv', 'L0_attn_wo', 'L0_ffn_W_base', 'L0_ffn_b_base',
        'L0_ffn_W_router', 'L0_ffn_A_stack', 'L0_ffn_B_stack']


def _shape_constants():
    inv = 1.0 / THETA ** (np.arange(0, HD, 2)[:HD // 2].astype(np.float32) / HD)
    angle = np.outer(np.arange(S), inv).astype(np.float32)
    pair = (np.arange(P) % HD) // 2
    sign = np.where(np.arange(P) % 2 == 0, -1.0, 1.0).astype(np.float32)
    cos_t = np.ascontiguousarray(np.cos(angle).T[pair]).astype(np.float32)
    sin_t = np.ascontiguousarray(np.sin(angle).T[pair] * sign[:, None]).astype(np.float32)
    consts = np.zeros((P, 3 * P + E), np.float32)
    consts[:, 0:P] = np.eye(P)
    row, col = np.arange(P)[:, None], np.arange(P)[None, :]
    consts[:, P:2 * P] = np.where(col > row, MASKED, 0.0)
    consts[:, 2 * P:3 * P] = np.where(row > col, MASKED, 0.0)
    consts[:, 3 * P:] = np.arange(E)
    return {"cos_t": cos_t, "sin_t": sin_t, "consts": consts}


def kernel(**inputs):
    import concourse.bacc as bacc
    from concourse.bass_utils import run_bass_kernel_spmd

    nc = bacc.Bacc("TRN2", target_bir_lowering=False, num_devices=1)
    arrays = {f"in_{name}": np.ascontiguousarray(inputs[name]) for name in _INS}
    arrays.update(_shape_constants())
    args = [nc.dram_tensor(n, a.shape, mybir.dt.from_np(a.dtype), kind="ExternalInput").ap() for n, a in arrays.items()]
    args.append(nc.dram_tensor("out", (B, S, D), F32, kind="ExternalOutput").ap())
    preln_block(nc, *args)
    r = run_bass_kernel_spmd(nc, [arrays], core_ids=[0])
    return r.results[0]["out"]
```

```python
from contextlib import ExitStack

import numpy as np

import concourse.bass as bass
from concourse import mybir

F32 = mybir.dt.float32
BF16 = mybir.dt.bfloat16
U32 = mybir.dt.uint32
ACT = mybir.ActivationFunctionType
ALU = mybir.AluOpType
AX = mybir.AxisListType

P = 128
B, S, D = 2, 1024, 512
H, HD = 32, 16
E, R = 8, 16
ER = E * R
KT = D // P
CHUNK = 512
CHUNKS = S // CHUNK
TPC = CHUNK // P
NCH = B * CHUNKS
QH = 4
NG = H // QH
ROUNDS = B * NG
GW = QH * HD
TT = S // P
PARTS = 3
SLOTS = 6
KROWS = SLOTS * HD
MROWS = KROWS + 2
THETA = 10000.0
EPS = 1e-5
SCALE = float(HD) ** -0.5
LORA_SCALE = 32.0 / R
MASKED = -1e30
RING = 3
G3 = 4
PC = 4
TRIPS3 = B * TT // G3
STAGED = 16 * (5 + KT)


def max_tasks():
    tasks = []
    for i in [*range(TPC, TT), *range(TPC)]:
        width = (i + 1) * P
        for part, w in enumerate([min(width, CHUNK)] + ([width - CHUNK] if width > CHUNK else [])):
            per = min(QH, CHUNK // w)
            per = 1 if per == 3 else per
            for h in range(0, QH, per):
                tasks.append((i, part, h, per, w))
    return tasks


def preln_block(nc, x, wq, wk, wv, wo, w_base, b_base, w_router, a_stack, b_stack, cos_t, sin_t, consts, out):
    tasks = max_tasks()
    NT = len(tasks)
    units = [(1, j) for j in range(TT)] + [(0, j) for j in range(TPC)]
    NU = len(units)
    assert NU % RING == 0 and NT % 2 == 0 and ROUNDS % RING == 1
    last_of = {1: TT - 1, 0: TPC - 1}
    width = [CHUNK - max(0, j - c * TPC) * P for c, j in units]
    pieces_of_work = [(u, k) for u in range(1, NU) for k in range(3)]
    spans = [width[u] if k < 2 else width[u - 1] for u, k in pieces_of_work]
    LATE = sum(t[0] >= TPC for t in tasks)
    extras, turn_of, given = {}, {}, 0
    for k, piece in enumerate(pieces_of_work):
        upto = NT * sum(spans[:k + 1]) // sum(spans)
        here = []
        for f in range(given, upto):
            here.append(f)
            if f == LATE + 2:
                here.append("M1")
        if piece == (TT + 1, 2):
            here.append("O0")
        given = upto
        extras[piece] = here
    extras["end"] = ["M0", "O1"]
    order = [e for here in extras.values() for e in here]
    turn_of = {e: k for k, e in enumerate(order)}
    TURNS = len(order)
    FIRST_TURNS = NT + 2
    BANKS = 3
    assert given == NT and TURNS % BANKS == 0

    with ExitStack() as ctx:
        def sb(name, shape, dt=F32):
            return ctx.enter_context(nc.sbuf_tensor(name, shape, dt))

        def sem(name):
            return ctx.enter_context(nc.semaphore(name))

        v_all = sb("v_all", [P, TT, ROUNDS * GW])
        att = sb("att", [P, TT, ROUNDS * GW])
        cst = sb("cst", [P, 3 * P + E])
        ident_b = sb("ident_b", [P, P], BF16)
        mask_q = sb("mask_q", [P, P], BF16)
        mask_k = sb("mask_k", [P, P], BF16)
        wo_sb = sb("wo_sb", [P, KT, D])
        wbT = sb("wbT", [P, KT, D])
        arT = sb("arT", [P, KT, ER + E])
        bT = sb("bT", [P, D])
        bias = sb("bias", [P, D])
        small = sb("small", [P, 280])
        mxp = sb("mxp", [P, QH, TPC, 2])
        nm = sb("nm", [P, CHUNKS, QH, TPC])
        mrow = sb("mrow", [P, CHUNKS, 2, P], BF16)
        rc = sb("rc", [P, 2, TPC, QH])
        ident = cst[:, 0:P]
        iota = cst[:, 3 * P:3 * P + E]
        KB = 256
        arena = sb("arena", [P, 100 * KB])

        def region(at, n):
            return arena[:, int(at * KB):int((at + n) * KB)]

        wqkv = region(0, 24).rearrange("p (w k n) -> p w k n", w=3, k=KT)
        xin = region(24, 16).rearrange("p (c t d) -> p c t d", c=2, t=TPC)
        xT = region(40, 16).rearrange("p (c k n) -> p c k n", c=2, k=KT)
        cs = region(56, 8).rearrange("p (w n) -> p w n", w=2)
        qf, t1, sw, t2, ro, r1 = (region(64 + 4 * k, 4).rearrange("p (s n) -> p s n", s=2) for k in range(6))
        pc = region(88, 12).bitcast(BF16).rearrange("p (s a n) -> p s a n", s=PC, a=PARTS)

        qs = region(0, 24).bitcast(BF16).rearrange("p (s c h n) -> p s c h n", s=RING, c=CHUNKS, h=QH)
        ks = region(24, 24).bitcast(BF16).rearrange("p (s h n) -> p s h n", s=RING, h=QH)
        pr = region(48, 24).rearrange("p (s h n) -> p s h n", s=RING, h=QH)
        vs = region(72, 12).rearrange("p (s j h d) -> p s j h d", s=RING, j=TT, h=QH)
        ot = region(84, 4).rearrange("p (c n) -> p c n", c=2)

        xr = region(0, 32).rearrange("p (j b d) -> p j b d", j=TT, b=B)
        at3, x1, xn, y3 = (region(32 + 8 * k, 8).rearrange("p (u n) -> p u n", u=G3) for k in range(4))
        attT, xnT = (region(64 + 4 * k, 4).rearrange("p (u k n) -> p u k n", u=2, k=KT) for k in range(2))
        h3 = region(72, 2).rearrange("p (u n) -> p u n", u=G3)
        hT = region(74, 1).rearrange("p (u n) -> p u n", u=2)
        attf = att[:].rearrange("p t n -> p (t n)")
        wb_st = attf[:, 0:KT * D].rearrange("p (o n) -> p o n", o=KT)
        a_st = attf[:, 2048:2560]
        b_st = attf[:, 2560:3072].rearrange("p (o e r) -> p o e r", o=KT, e=E)
        r_st = attf[0:E, 3072:3584]

        ps = ctx.enter_context(nc.psum_tensor("ps", [P, 8, 512], F32))
        pieces = nc.dram_tensor("pieces", [2, PARTS, ROUNDS, QH, HD, S], BF16).ap()

        stats = small[:, 0:24].rearrange("p (t n) -> p t n", t=4)
        mv = small[:, 24:32].rearrange("p (t n) -> p t n", t=4)
        veps = small[:, 32:36]
        rstd = small[:, 36:40]
        mhalf = small[:, 40:44]
        top = small[:, 48:80].rearrange("p (u n) -> p u n", u=4)
        topi = small[:, 80:112].bitcast(U32).rearrange("p (u n) -> p u n", u=4)
        idxf = small[:, 112:120].rearrange("p (u n) -> p u n", u=4)
        gap = small[:, 120:124]
        ex = small[:, 124:128]
        den = small[:, 128:132]
        w0 = small[:, 132:136]
        w1 = small[:, 136:140]
        comb0 = small[:, 144:176].rearrange("p (u n) -> p u n", u=4)
        comb = small[:, 176:208].rearrange("p (u n) -> p u n", u=4)
        lg = small[:, 208:240].rearrange("p (u n) -> p u n", u=4)
        comb1 = small[:, 240:272].rearrange("p (u n) -> p u n", u=4)

        consts_loaded, weights_loaded, staged = sem("consts_loaded"), sem("weights_loaded"), sem("staged")
        tables_loaded = sem("tables_loaded")
        x_loaded = [sem(f"x_loaded{c}") for c in range(2)]
        consts_ready, half_ready = sem("consts_ready"), sem("half_ready")
        aggr_done, rstd_ready, xn_ready = sem("aggr_done"), sem("rstd_ready"), sem("xn_ready")
        carried = sem("carried")
        stats_done, eps_added = sem("stats_done"), sem("eps_added")
        m1_ready, rc_ready = sem("m1_ready"), sem("rc_ready")
        dve_step = sem("dve_step")
        tp_ready, xT_ready = sem("tp_ready"), sem("xT_ready")
        qk_ready, qf_ready = sem("qk_ready"), sem("qf_ready")
        v_ready, v_copied = sem("v_ready"), sem("v_copied")
        t1_ready, ro_ready, p1_ready, r1_ready, p2_ready, p3_ready = (
            sem(n) for n in ("t1_ready", "ro_ready", "p1_ready", "r1_ready", "p2_ready", "p3_ready"))
        stored = [sem(f"stored{s}") for s in range(PC)]
        wt_ready, wt_copied = sem("wt_ready"), sem("wt_copied")
        ones_set, vs_ready = sem("ones_set"), sem("vs_ready")
        stack_loaded = [sem(f"stack_loaded{s}") for s in range(RING)]
        rows_loaded = [sem(f"rows_loaded{c}") for c in range(CHUNKS)]
        bank_filled, bank_emptied = sem("bank_filled"), sem("bank_emptied")
        late_reduced, nm_ready = sem("late_reduced"), sem("nm_ready")
        k_scores, exp_done, pv_done = sem("k_scores"), sem("exp_done"), sem("pv_done")
        o_copied = sem("o_copied")
        xr_loaded, at_ready = sem("xr_loaded"), sem("at_ready")
        tr_ready, tr_copied = sem("tr_ready"), sem("tr_copied")
        mm_ready, mm_read = sem("mm_ready"), sem("mm_read")
        x1_ready, aggr3, eps3, rstd3, xn3 = (sem(n) for n in ("x1_ready", "aggr3", "eps3", "rstd3", "xn3"))
        x1b_ready, gap_ready, ex_ready, h_ready = (sem(n) for n in ("x1b_ready", "gap_ready", "ex_ready", "h_ready"))
        y_psum, y_read, y_stored = sem("y_psum"), sem("y_read"), sem("y_stored")

        TP, QK, VP = (0, 1), (2, 3, 4, 5), (6, 7)
        KS_BANK, RING_BANK, O_BANK = 0, 4, 7
        BASE, TR, MM = 0, 4, 6

        ATT_DONE = BANKS + FIRST_TURNS + (ROUNDS - 1) * TURNS + 2

        def turn(n, e):
            if isinstance(n, int) and n == -1:
                return e if e in range(NT) else NT + ("M1", "M0").index(e)
            if isinstance(n, int) and n == ROUNDS - 1:
                return FIRST_TURNS + TURNS * n + ("O0", "O1").index(e)
            return n * TURNS + (FIRST_TURNS + turn_of[e])

        def ring_bank(n, e):
            if isinstance(n, int):
                return RING_BANK + turn(n, e) % BANKS
            return RING_BANK + (FIRST_TURNS + turn_of[e]) % BANKS

        def alone(eng):
            eng.sem_inc(carried, 1)

        block = ctx.enter_context(nc.Block())
        xrows = x.rearrange("b (c t p) d -> (b c) p t d", c=CHUNKS, p=P)

        @block.sync
        def _(sp):
            for done in (*stored, y_stored):
                sp.sem_inc(done, 16)
            sp.dma_start(cst[:], consts).then_inc(consts_loaded, 16)
            sp.dma_start(xin[:, 0], xrows[0]).then_inc(x_loaded[0], 16)
            for w, src in enumerate((wq, wk, wv)):
                sp.dma_start(wqkv[:, w], src.rearrange("(k p) n -> p k n", p=P)).then_inc(weights_loaded, 16)
            sp.dma_start(cs[:, 0], cos_t).then_inc(tables_loaded, 16)
            sp.dma_start(cs[:, 1], sin_t).then_inc(tables_loaded, 16)
            sp.dma_start(xin[:, 1], xrows[1]).then_inc(x_loaded[1], 16)
            sp.dma_start(wo_sb[:], wo.rearrange("(k p) n -> p k n", p=P)).then_inc(staged, 16)
            sp.dma_start(wb_st, w_base.rearrange("(o p) n -> p o n", p=P)).then_inc(staged, 16)
            sp.dma_start(a_st, a_stack.rearrange("e r n -> (e r) n")).then_inc(staged, 16)
            sp.dma_start(r_st, w_router).then_inc(staged, 16)
            for o in range(KT):
                sp.dma_start(b_st[:, o], b_stack[:, o * P:(o + 1) * P, :].rearrange("e p r -> p e r")).then_inc(staged, 16)
            sp.dma_start(bias[:], b_base.partition_broadcast(P)).then_inc(staged, 16)

            for k in range(NCH):
                b, c = k // CHUNKS, k % CHUNKS
                for m in range(2 * KT):
                    t = 2 * KT * k + m
                    sp.wait_ge(p3_ready, 2 + t + 1)
                    dst = pieces[m // KT].rearrange("a n h d t -> (n h d) a t")
                    row = b * NG * GW + (m % KT) * P
                    sp.dma_start(dst[row:row + P, :, c * CHUNK:(c + 1) * CHUNK], pc[:, t % PC]).then_inc(stored[t % PC], 16)
                    if m == 0 and k + 1 < NCH and k >= 1:
                        sp.wait_ge(tp_ready, TPC * k)
                        sp.dma_start(xin[:, (k + 1) % 2], xrows[k + 1]).then_inc(x_loaded[(k + 1) % 2], 16)

            for s in range(PC):
                sp.wait_ge(stored[s], 16 * (1 + NCH * 2 * KT // PC))
            sp.wait_ge(v_copied, 2 + TPC * NCH)

            def load_round(n, s):
                for qk, dst, use in ((0, qs, (0, 0, 0, 1, 1, 2)), (1, ks, (0, 1, 2, 0, 1, 0))):
                    for slot, part in enumerate(use):
                        src = pieces[qk, part].rearrange("n h d t -> d n h t")[:, bass.ds(n, 1)].rearrange("d n h t -> d (n h) t")
                        if qk == 0:
                            src = src.rearrange("d h (c t) -> d c h t", c=CHUNKS)
                        sp.dma_start(dst[HD * slot:HD * (slot + 1), s], src).then_inc(stack_loaded[s], 16)

            def load_rows(n, s):
                for c, e in ((1, "M1"), (0, "M0")):
                    sp.wait_ge(bank_emptied, BANKS + turn(n - 1, e) + 1)
                    for a in range(2):
                        sp.dma_start(qs[KROWS + a:KROWS + a + 1, s, c].rearrange("p h (i t) -> p (h i) t", t=P),
                                     mrow[0:QH * TPC, c, a, :]).then_inc(rows_loaded[c], 16)

            for n in range(RING):
                load_round(n, n)
            load_rows(0, 0)
            with sp.Fori(0, (ROUNDS - 1) // RING - 1) as i:
                for u in range(RING):
                    n = i * RING + u
                    load_rows(n + 1, (u + 1) % RING)
                    sp.wait_ge(pv_done, RING + NU * (n + 1))
                    load_round(n + RING, u)
            for n in range(ROUNDS - 1 - RING, ROUNDS - 1):
                load_rows(n + 1, (n + 1) % RING)
                if n + RING < ROUNDS:
                    sp.wait_ge(pv_done, RING + NU * (n + 1))
                    load_round(n + RING, n % RING)

            sp.wait_ge(bank_emptied, ATT_DONE)
            for b in range(B):
                sp.dma_start(xr[:, :, b], x[b].rearrange("(j p) d -> p j d", p=P)).then_inc(xr_loaded, 16)
            with sp.Fori(0, TRIPS3) as i:
                for u in range(G3):
                    sp.wait_ge(y_read, G3 + i * G3 + u + 1)
                    dst = out[u % B].rearrange("(j p) d -> p j d", p=P)[:, bass.ds(i * (G3 // B) + u // B, 1)]
                    sp.dma_start(dst.rearrange("p j d -> p (j d)"), y3[:, u]).then_inc(y_stored, 16)
            sp.wait_ge(y_stored, 16 + 16 * B * TT)

        @block.gpsimd
        def _(pool):
            nc.gpsimd.memset(mhalf, -0.5).then_inc(half_ready, 1)
            pool.sem_inc(p3_ready, 2)
            pool.wait_ge(tables_loaded, 32)
            pool.wait_ge(half_ready, 1)
            with pool.Fori(0, B) as b:
                for c in range(CHUNKS):
                    k = b * CHUNKS + c
                    pool.wait_ge(aggr_done, k + 1)
                    alone(pool)
                    nc.gpsimd.tensor_scalar(veps, mv[:, :, 1], EPS, 1.0, ALU.add, ALU.mult).then_inc(eps_added, 1)
                    pool.wait_ge(eps_added, k + 1)
                    nc.gpsimd.tensor_tensor(rstd, veps, mhalf, ALU.pow).then_inc(rstd_ready, 1)
                    for m in range(2 * KT + 2):
                        t = k * 2 * KT + m
                        if m < 2 * KT:
                            pool.wait_ge(qf_ready, t + 1)
                            nc.gpsimd.tensor_tensor(t1[:, m % 2], qf[:, m % 2], cs[:, 0, c * CHUNK:(c + 1) * CHUNK],
                                                    ALU.mult).then_inc(t1_ready, 1)
                        if m >= 2:
                            pool.wait_ge(p2_ready, t - 1)
                            v = (m - 2) % PC
                            nc.gpsimd.tensor_tensor(pc[:, v, 2], r1[:, m % 2], pc[:, v, 1], ALU.subtract).then_inc(p3_ready, 1)

            pool.wait_ge(v_copied, 2 + TPC * NCH)
            for s in range(PC):
                pool.wait_ge(stored[s], 16 * (1 + NCH * 2 * KT // PC))
            nc.gpsimd.memset(ks[KROWS:MROWS], 1.0).then_inc(ones_set, 1)
            pool.wait_ge(ones_set, 1)
            nc.gpsimd.memset(vs[:, :, :, :, HD:2 * HD], 1.0).then_inc(ones_set, 1)

            def gather_v(n, s):
                src = v_all[:, :, bass.ds(n * GW, GW)].rearrange("p j (h d) -> p j h d", h=QH)
                nc.gpsimd.tensor_copy(vs[:, s, :, :, 0:HD], src).then_inc(vs_ready, 1)

            for n in range(RING):
                gather_v(n, n)
            with pool.Fori(0, (ROUNDS - 1) // RING - 1) as i:
                for u in range(RING):
                    n = i * RING + u
                    pool.wait_ge(pv_done, RING + NU * (n + 1))
                    gather_v(n + RING, u)
            pool.wait_ge(pv_done, RING + NU * (ROUNDS - RING))
            gather_v(ROUNDS - 1, (ROUNDS - 1) % RING)

            pool.wait_ge(bank_emptied, ATT_DONE)
            with pool.Fori(0, TRIPS3) as i:
                for u in range(G3):
                    t = i * G3 + u
                    if u == 0:
                        pool.wait_ge(x1b_ready, i + 1)
                    nc.gpsimd.tensor_copy(at3[:, u], attf[:, bass.ds(i * (G3 * D) + u * D, D)]).then_inc(at_ready, 1)
                for u in range(G3):
                    t = i * G3 + u
                    pool.wait_ge(aggr3, t + 1)
                    alone(pool)
                    nc.gpsimd.tensor_scalar(veps[:, u:u + 1], mv[:, u, 1:2], EPS, 1.0, ALU.add, ALU.mult).then_inc(eps3, 1)
                    pool.wait_ge(eps3, t + 1)
                    nc.gpsimd.tensor_tensor(rstd[:, u:u + 1], veps[:, u:u + 1], mhalf[:, 0:1], ALU.pow).then_inc(rstd3, 1)

        @block.scalar
        def _(act):
            act.sem_inc(v_copied, 2)
            with act.Fori(0, B) as b:
                for c in range(CHUNKS):
                    k = b * CHUNKS + c
                    for t in range(TPC):
                        act.wait_ge(tp_ready, k * TPC + t + 1)
                        nc.scalar.copy(xT[:, c, :, t * P:(t + 1) * P], ps[:, TP[t % 2]].rearrange("p (k n) -> p k n", k=KT)).then_inc(
                            xT_ready, 1)
                    for m in range(2 * KT + 2):
                        t = k * 2 * KT + m
                        if m < 2 * KT:
                            act.wait_ge(qk_ready, t + 1)
                            nc.scalar.copy(qf[:, m % 2], ps[:, QK[m % 4]]).then_inc(qf_ready, 1)
                        if 1 <= m <= 2 * KT:
                            v = (m - 1) % PC
                            act.wait_ge(ro_ready, t)
                            act.wait_ge(stored[v], 16 + 16 * (k * (2 * KT // PC) + (m - 1) // PC))
                            nc.scalar.copy(pc[:, v, 0], ro[:, (m - 1) % 2]).then_inc(p1_ready, 1)
                        if m >= 2:
                            act.wait_ge(r1_ready, t - 1)
                            nc.scalar.copy(pc[:, (m - 2) % PC, 1], r1[:, m % 2]).then_inc(p2_ready, 1)
                    for t in range(TPC):
                        act.wait_ge(v_ready, k * TPC + t + 1)
                        nc.scalar.copy(v_all[:, c * TPC + t, bass.ds(b * D, D)], ps[:, VP[t % 2]]).then_inc(v_copied, 1)

            def exps(n, u, slot):
                c, j = units[u]
                w = CHUNK - max(0, j - c * TPC) * P
                for hp in range(2):
                    act.wait_ge(k_scores, 2 * NU * n + 2 * u + hp + 1)
                    if hp == 0:
                        act.wait_ge(pv_done, NU * n + u + 1)
                    nc.scalar.activation(pr[:, slot, 2 * hp:2 * hp + 2, 0:w], ps[:, KS_BANK + 2 * hp:KS_BANK + 2 * hp + 2, 0:w],
                                         ACT.Exp, scale=SCALE).then_inc(exp_done, 1)

            def ot_free(n, cc):
                e = ("O0", "O1")[cc]
                return FIRST_TURNS if isinstance(n, int) and n == 0 else TURNS * (n - 1) + (FIRST_TURNS + turn_of[e] + 1)

            def copy_output(n, cc, done):
                act.wait_ge(pv_done, RING + NU * n + done)
                act.wait_ge(bank_filled, ot_free(n, cc))
                nc.scalar.copy(ot[:, cc], ps[:, O_BANK]).then_inc(o_copied, 1)

            def act_round(n):
                for u in range(NU):
                    exps(n, u, u % RING)
                    if u == TT:
                        copy_output(n, 0, TT)
                copy_output(n, 1, NU)

            act.sem_inc(exp_done, 2)
            act.sem_inc(o_copied, 1)
            with act.Fori(0, (ROUNDS - 1) // RING) as i:
                for u in range(RING):
                    act_round(i * RING + u)
            act_round(ROUNDS - 1)

            act.wait_ge(bank_emptied, ATT_DONE)
            act.sem_inc(tr_copied, 2)
            with act.Fori(0, TRIPS3) as i:
                def copy_tr(y, dst, shape=None):
                    act.wait_ge(tr_ready, i * 3 * G3 + y + 1)
                    src = ps[:, TR + y % 2]
                    src = src.rearrange("p (k n) -> p k n", k=KT) if shape is None else src[:, 0:shape]
                    nc.scalar.copy(dst, src).then_inc(tr_copied, 1)

                def router_exp(u):
                    act.wait_ge(gap_ready, i * G3 + u + 1)
                    nc.scalar.activation(ex[:, u:u + 1], gap[:, u:u + 1], ACT.Exp).then_inc(ex_ready, 1)

                for u in range(G3):
                    copy_tr(u, attT[:, u % 2])
                for u in range(G3):
                    copy_tr(G3 + u, xnT[:, u % 2])
                    if u >= 1:
                        router_exp(u - 1)
                router_exp(G3 - 1)
                for u in range(G3):
                    copy_tr(2 * G3 + u, hT[:, u % 2], P)

        @block.vector
        def _(dve):
            steps = [0]

            def link(ins, base):
                steps[0] += 1
                ins.then_inc(dve_step, 1)
                dve.wait_ge(dve_step, base + steps[0])

            dve.wait_ge(consts_loaded, 16)
            nc.vector.tensor_copy(ident_b[:], ident)
            nc.vector.tensor_copy(mask_q[:], cst[:, P:2 * P])
            nc.vector.tensor_copy(mask_k[:], cst[:, 2 * P:3 * P]).then_inc(consts_ready, 1)
            dve.wait_ge(tables_loaded, 32)
            swap = [l ^ 1 for l in range(32)]
            per1 = 2 * (2 * KT)
            with dve.Fori(0, B) as b:
                for c in range(CHUNKS):
                    k = b * CHUNKS + c
                    dve.wait_ge(x_loaded[c], 16 * (b + 1))
                    for t in range(TPC):
                        nc.vector.bn_stats(stats[:, t], xin[:, c, t]).then_inc(stats_done, 1)
                    for t in range(TPC):
                        dve.wait_ge(stats_done, k * TPC + t + 1)
                        alone(dve)
                        last = nc.vector.bn_aggr(mv[:, t], stats[:, t])
                    last.then_inc(aggr_done, 1)
                    dve.wait_ge(rstd_ready, k + 1)
                    for t in range(TPC):
                        nc.vector.tensor_scalar(xin[:, c, t], xin[:, c, t], mv[:, t, 0:1], rstd[:, t:t + 1],
                                                ALU.subtract, ALU.mult).then_inc(xn_ready, 1)
                    for m in range(2 * KT + 1):
                        t = k * 2 * KT + m
                        s = m % 2
                        if m < 2 * KT:
                            dve.wait_ge(qf_ready, t + 1)
                            alone(dve)
                            link(nc.vector.stream_shuffle(sw[:, s], qf[:, s], swap), b * CHUNKS * per1)
                            link(nc.vector.tensor_tensor(t2[:, s], sw[:, s], cs[:, 1, c * CHUNK:(c + 1) * CHUNK], ALU.mult),
                                 b * CHUNKS * per1)
                            dve.wait_ge(t1_ready, t + 1)
                            nc.vector.tensor_tensor(ro[:, s], t1[:, s], t2[:, s], ALU.add).then_inc(ro_ready, 1)
                        if m >= 1:
                            v = (m - 1) % 2
                            dve.wait_ge(p1_ready, t)
                            dve.wait_ge(p3_ready, t)
                            nc.vector.tensor_tensor(r1[:, v], ro[:, v], pc[:, (m - 1) % PC, 0], ALU.subtract).then_inc(r1_ready, 1)
            assert steps[0] == CHUNKS * per1
            steps[0] = 0
            base2 = NCH * per1

            for g, dst in enumerate([wbT[:, k] for k in range(KT)] + [arT[:, :, 0:ER], arT[:, :, ER:ER + E], bT[:]]):
                dve.wait_ge(wt_ready, g + 1)
                src = ps[:, TP[g % 2]]
                if g == KT:
                    src = src.rearrange("p (k n) -> p k n", k=KT)
                if g == KT + 1:
                    src = src[:, 0:KT * E].rearrange("p (k n) -> p k n", k=KT)
                nc.vector.tensor_copy(dst, src).then_inc(wt_copied, 1)

            dve.sem_inc(bank_emptied, BANKS)

            def maximum(n, e, m):
                i, part, h, per, w = tasks[e]
                dve.wait_ge(bank_filled, turn(n, e) + 1)
                src = ps[:, ring_bank(n, e), 0:per * w].rearrange("p (h n) -> p h n", h=per)
                if i < TPC:
                    nc.vector.tensor_reduce(nm[:, 0, h:h + per, i], src, AX.X, ALU.max, negate=True).then_inc(bank_emptied, 1)
                else:
                    nc.vector.tensor_reduce(mxp[:, h:h + per, i - TPC, part], src, AX.X, ALU.max).then_inc(bank_emptied, 1)
                    if e == LATE - 1:
                        dve.wait_ge(bank_emptied, BANKS + turn(n, e) + 1)
                        nc.vector.tensor_reduce(nm[:, 1], mxp[:], AX.X, ALU.max, negate=True).then_inc(nm_ready, 1)

            def split_rows(n, e, m):
                c = ("M0", "M1").index(e)
                dve.wait_ge(bank_filled, turn(n, e) + 1)
                if not (isinstance(m, int) and m == 0):
                    dve.wait_ge(rows_loaded[c], m * 32)
                rows = ps[0:QH * TPC, ring_bank(n, e), 0:P]
                nc.vector.tensor_copy(mrow[0:QH * TPC, c, 0], rows).then_inc(m1_ready, 1)
                dve.wait_ge(m1_ready, 2 * m + 2 - c)
                nc.vector.tensor_tensor(mrow[0:QH * TPC, c, 1], rows, mrow[0:QH * TPC, c, 0], ALU.subtract).then_inc(
                    bank_emptied, 1)

            def normalise(n, e):
                cc = ("O0", "O1").index(e)
                c = units[0][0] if cc == 0 else units[-1][0]
                dve.wait_ge(bank_filled, turn(n, e) + 1)
                o = ps[:, ring_bank(n, e)].rearrange("p (t h d) -> p t h d", t=TPC, h=QH)
                nc.vector.reciprocal(rc[:, cc], o[:, :, :, HD]).then_inc(rc_ready, 1)
                dve.wait_ge(rc_ready, 2 * n + cc + 1)
                dst = att[:, c * TPC:(c + 1) * TPC, bass.ds(n * GW, GW)].rearrange("p t (h d) -> p t h d", h=QH)
                nc.vector.tensor_tensor(dst, o[:, :, :, 0:HD], rc[:, cc].unsqueeze(3).broadcast_to([P, TPC, QH, HD]),
                                        ALU.mult).then_inc(bank_emptied, 1)

            for e in [*range(NT), "M1", "M0"]:
                split_rows(-1, e, 0) if e in ("M1", "M0") else maximum(-1, e, 0)
            with dve.Fori(0, (ROUNDS - 1) // RING) as i:
                for u in range(RING):
                    n = i * RING + u
                    for e in order:
                        if e in ("M1", "M0"):
                            split_rows(n, e, n + 1)
                        elif e in ("O0", "O1"):
                            normalise(n, e)
                        else:
                            maximum(n, e, n + 1)
            for e in ("O0", "O1"):
                normalise(ROUNDS - 1, e)

            dve.sem_inc(mm_read, 2)
            dve.sem_inc(y_read, G3)
            dve.sem_inc(x1b_ready, 1)
            dve.wait_ge(xr_loaded, 16 * B)
            dve.wait_ge(staged, STAGED)
            xrf = xr[:].rearrange("p j b d -> p (j b d)")

            def normal(i, u):
                dve.wait_ge(rstd3, i * G3 + u + 1)
                nc.vector.tensor_scalar(xn[:, u], x1[:, u], mv[:, u, 0:1], rstd[:, u:u + 1],
                                        ALU.subtract, ALU.mult).then_inc(xn3, 1)

            per3 = 11 * G3
            with dve.Fori(0, TRIPS3) as i:
                base = i * per3 + base2
                for u in range(G3):
                    dve.wait_ge(y_read, G3 + i * G3)
                    dve.wait_ge(mm_ready, i * 2 * G3 + u + 1)
                    nc.vector.tensor_tensor(x1[:, u], ps[:, MM + u % 2], xrf[:, bass.ds(i * (G3 * D) + u * D, D)],
                                            ALU.add).then_inc(mm_read, 1)
                    dve.wait_ge(mm_read, i * 2 * G3 + 2 + u + 1)
                    link(nc.vector.bn_stats(stats[:, u], x1[:, u]), base)
                    alone(dve)
                    nc.vector.bn_aggr(mv[:, u], stats[:, u]).then_inc(aggr3, 1)
                    if u >= 1:
                        normal(i, u - 1)
                normal(i, G3 - 1)
                for u in range(G3):
                    last = nc.vector.tensor_tensor(x1[:, u], x1[:, u], bias[:], ALU.add)
                last.then_inc(x1b_ready, 1)
                for u in range(G3):
                    dve.wait_ge(mm_ready, i * 2 * G3 + G3 + u + 1)
                    bank = ps[:, MM + u % 2]
                    link(nc.vector.tensor_copy(lg[:, u], bank[:, ER:ER + E]), base)
                    alone(dve)
                    link(nc.vector.max(top[:, u], lg[:, u]), base)
                    nc.vector.tensor_tensor(gap[:, u:u + 1], top[:, u, 1:2], top[:, u, 0:1], ALU.subtract).then_inc(gap_ready, 1)
                    link(nc.vector.max_index(topi[:, u], top[:, u], lg[:, u]), base)
                    link(nc.vector.tensor_copy(idxf[:, u], topi[:, u, 0:2]), base)
                    dve.wait_ge(ex_ready, i * G3 + u + 1)
                    link(nc.vector.tensor_scalar(den[:, u:u + 1], ex[:, u:u + 1], 1.0, 1.0 / LORA_SCALE, ALU.add, ALU.mult), base)
                    link(nc.vector.reciprocal(w0[:, u:u + 1], den[:, u:u + 1]), base)
                    link(nc.vector.tensor_tensor(w1[:, u:u + 1], w0[:, u:u + 1], ex[:, u:u + 1], ALU.mult), base)
                    link(nc.vector.tensor_scalar(comb0[:, u], iota, idxf[:, u, 0:1], w0[:, u:u + 1], ALU.is_equal, ALU.mult), base)
                    link(nc.vector.tensor_scalar(comb1[:, u], iota, idxf[:, u, 1:2], w1[:, u:u + 1], ALU.is_equal, ALU.mult), base)
                    link(nc.vector.tensor_tensor(comb[:, u], comb0[:, u], comb1[:, u], ALU.add), base)
                    nc.vector.tensor_tensor(h3[:, u].rearrange("p (e r) -> p e r", e=E),
                                            bank[:, 0:ER].rearrange("p (e r) -> p e r", e=E),
                                            comb[:, u].unsqueeze(2).broadcast_to([P, E, R]), ALU.mult).then_inc(mm_read, 1)
                dve.wait_ge(y_stored, 16 + i * (16 * G3))
                dve.wait_ge(x1b_ready, i + 2)
                for u in range(G3):
                    dve.wait_ge(y_psum, i * G3 + u + 1)
                    nc.vector.tensor_tensor(y3[:, u], ps[:, BASE + u], x1[:, u], ALU.add).then_inc(y_read, 1)
            assert steps[0] == per3, steps

        @block.tensor
        def _(pe):
            mm, tr = nc.tensor.matmul, nc.tensor.transpose
            pe.wait_ge(consts_loaded, 16)
            pe.wait_ge(weights_loaded, 48)
            with pe.Fori(0, B) as b:
                for c in range(CHUNKS):
                    k = b * CHUNKS + c
                    for t in range(TPC):
                        pe.wait_ge(xn_ready, k * TPC + t + 1)
                        if t >= 2:
                            pe.wait_ge(xT_ready, k * TPC + t - 1)
                        for kt in range(KT):
                            last = tr(ps[:, TP[t % 2], kt * P:(kt + 1) * P], xin[:, c, t, kt * P:(kt + 1) * P], ident)
                        last.then_inc(tp_ready, 1)
                    pe.wait_ge(xT_ready, k * TPC + TPC)
                    for m in range(2 * KT):
                        if m >= 4:
                            pe.wait_ge(qf_ready, k * 2 * KT + m - 3)
                        for kt in range(KT):
                            last = mm(ps[:, QK[m % 4]], wqkv[:, m // KT, kt, (m % KT) * P:(m % KT + 1) * P], xT[:, c, kt],
                                      start=kt == 0, stop=kt == KT - 1)
                        last.then_inc(qk_ready, 1)
                    for t in range(TPC):
                        pe.wait_ge(v_copied, k * TPC + t + 1)
                        for kt in range(KT):
                            last = mm(ps[:, VP[t % 2]], xT[:, c, kt, t * P:(t + 1) * P], wqkv[:, 2, kt],
                                      start=kt == 0, stop=kt == KT - 1)
                        last.then_inc(v_ready, 1)
                    pe.wait_ge(qf_ready, k * 2 * KT + 2 * KT)

            pe.wait_ge(staged, STAGED)
            for g in range(KT + 3):
                if g >= 2:
                    pe.wait_ge(wt_copied, g - 1)
                bank = ps[:, TP[g % 2]]
                for o in range(KT):
                    if g < KT:
                        last = tr(bank[:, o * P:(o + 1) * P], wb_st[:, o, g * P:(g + 1) * P], ident)
                    elif g == KT:
                        last = tr(bank[:, o * P:(o + 1) * P], a_st[:, o * P:(o + 1) * P], ident)
                    elif g == KT + 1:
                        last = tr(bank[:, o * E:(o + 1) * E], r_st[:, o * P:(o + 1) * P], cst[0:E, 0:E])
                    else:
                        last = tr(bank[:, o * P:(o + 1) * P], b_st[:, o].rearrange("p e r -> p (e r)"), ident)
                last.then_inc(wt_ready, 1)
            pe.wait_ge(wt_copied, KT + 3)
            pe.wait_ge(v_copied, 2 + NCH * TPC)

            pe.wait_ge(consts_ready, 1)
            pe.wait_ge(ones_set, 2)

            def extra(n, s, e):
                bank = ring_bank(n, e)
                pe.wait_ge(bank_emptied, turn(n, e) + 1)
                if e in ("M1", "M0"):
                    c = ("M0", "M1").index(e)
                    if c == 1:
                        pe.wait_ge(nm_ready, n + 2)
                    else:
                        pe.wait_ge(bank_emptied, BANKS + turn(n, NT - 1) + 1)
                    last = tr(ps[0:QH * TPC, bank, 0:P], nm[:, c].rearrange("p h i -> p (h i)"), ident)
                elif e in ("O0", "O1"):
                    cc = ("O0", "O1").index(e)
                    pe.wait_ge(o_copied, 2 * n + cc + 2)
                    for t in range(TPC):
                        last = tr(ps[:, bank, t * P:(t + 1) * P], ot[:, cc, t * P:(t + 1) * P], ident)
                else:
                    i, part, h0, per, w = tasks[e]
                    v = (s + 1) % RING
                    diagonal = part * CHUNK + w == (i + 1) * P
                    for h in range(per):
                        o = ps[:, bank, h * w:(h + 1) * w]
                        last = mm(o, qs[0:KROWS, v, i // TPC, h0 + h, i % TPC * P:(i % TPC + 1) * P],
                                  ks[0:KROWS, v, h0 + h, part * CHUNK:part * CHUNK + w], start=True, stop=not diagonal)
                        if diagonal:
                            last = mm(o[:, w - P:w], ident_b[:], mask_q[:], start=False, stop=True)
                last.then_inc(bank_filled, 1)

            def times_v(n, s, u):
                c, j = units[u]
                q0 = max(0, j - c * TPC) * P
                pe.wait_ge(exp_done, 2 + 2 * NU * n + 2 * u + 2)
                if u == 0:
                    pe.wait_ge(vs_ready, n + 1)
                if j == 0:
                    pe.wait_ge(o_copied, 2 * n + (u > 0) + 1)
                for h in range(QH):
                    last = mm(ps[2 * HD * h:2 * HD * (h + 1), O_BANK, q0:CHUNK], vs[:, s, j, h], pr[:, u % RING, h, 0:CHUNK - q0],
                              start=j == 0, stop=j == last_of[c])
                last.then_inc(pv_done, 1)

            def key_scores(n, s, u, hp):
                c, j = units[u]
                q0 = CHUNK - width[u]
                pe.wait_ge(exp_done, 2 * NU * n + 2 * u + hp + 1)
                for h in (2 * hp, 2 * hp + 1):
                    diagonal = j >= c * TPC
                    o = ps[:, KS_BANK + h]
                    last = mm(o[:, 0:width[u]], ks[0:MROWS, s, h, j * P:(j + 1) * P], qs[0:MROWS, s, c, h, q0:CHUNK],
                              start=True, stop=not diagonal)
                    if diagonal:
                        last = mm(o[:, 0:P], ident_b[:], mask_k[:], start=False, stop=True)
                last.then_inc(k_scores, 1)

            def first_scores(n, s):
                pe.wait_ge(rows_loaded[1], 32 * n + 32)
                for hp in range(2):
                    key_scores(n, s, 0, hp)

            def pe_round(n, s, following=True):
                if following:
                    loads = 16 * 2 * SLOTS
                    pe.wait_ge(stack_loaded[(s + 1) % RING], (n - s) * (loads // RING) + loads * (1 + (s == RING - 1)))
                for u in range(1, NU):
                    if u == TT:
                        pe.wait_ge(rows_loaded[0], 32 * n + 32)
                    for k in range(3):
                        if k < 2:
                            key_scores(n, s, u, k)
                        else:
                            times_v(n, s, u - 1)
                        for e in extras[u, k]:
                            if following or e == "O0":
                                extra(n, s, e)
                times_v(n, s, NU - 1)
                if following:
                    first_scores(n + 1, (s + 1) % RING)
                for e in extras["end"]:
                    if following or e == "O1":
                        extra(n, s, e)

            pe.sem_inc(pv_done, RING)
            pe.wait_ge(stack_loaded[0], 16 * 2 * SLOTS)
            for e in [*range(NT), "M1", "M0"]:
                extra(-1, -1, e)
            first_scores(0, 0)
            with pe.Fori(0, (ROUNDS - 1) // RING) as i:
                for u in range(RING):
                    pe_round(i * RING + u, u)
            pe_round(ROUNDS - 1, 0, False)

            pe.wait_ge(bank_emptied, ATT_DONE)
            with pe.Fori(0, TRIPS3) as i:
                def transposed(y, src):
                    pe.wait_ge(tr_copied, i * 3 * G3 + y + 1)
                    for kt, block_in in enumerate(src):
                        last = tr(ps[:, TR + y % 2, kt * P:(kt + 1) * P], block_in, ident)
                    last.then_inc(tr_ready, 1)

                def blocks(a):
                    return [a[:, kt * P:(kt + 1) * P] for kt in range(KT)]

                def project(u):
                    pe.wait_ge(tr_copied, i * 3 * G3 + 2 + u + 1)
                    pe.wait_ge(mm_read, i * 2 * G3 + u + 1)
                    for kt in range(KT):
                        last = mm(ps[:, MM + u % 2], attT[:, u % 2, kt], wo_sb[:, kt], start=kt == 0, stop=kt == KT - 1)
                    last.then_inc(mm_ready, 1)

                def dense(u):
                    pe.wait_ge(tr_copied, i * 3 * G3 + 2 + G3 + u + 1)
                    pe.wait_ge(mm_read, i * 2 * G3 + G3 + u + 1)
                    for kt in range(KT):
                        last = mm(ps[:, MM + u % 2, 0:ER + E], xnT[:, u % 2, kt], arT[:, kt], start=kt == 0, stop=kt == KT - 1)
                    last.then_inc(mm_ready, 1)
                    pe.wait_ge(y_read, i * G3 + u + 1)
                    for kt in range(KT):
                        mm(ps[:, BASE + u], xnT[:, u % 2, kt], wbT[:, kt], start=kt == 0, stop=False)

                for u in range(G3 + 1):
                    if u < G3:
                        pe.wait_ge(at_ready, i * G3 + u + 1)
                        transposed(u, blocks(at3[:, u]))
                    if u >= 1:
                        project(u - 1)
                for u in range(G3 + 1):
                    if u < G3:
                        pe.wait_ge(xn3, i * G3 + u + 1)
                        transposed(G3 + u, blocks(xn[:, u]))
                    if u >= 1:
                        dense(u - 1)
                for u in range(G3 + 1):
                    if u < G3:
                        pe.wait_ge(mm_read, i * 2 * G3 + 2 + G3 + u + 1)
                        transposed(2 * G3 + u, [h3[:, u]])
                    if u >= 1:
                        v = u - 1
                        pe.wait_ge(tr_copied, i * 3 * G3 + 2 + 2 * G3 + v + 1)
                        mm(ps[:, BASE + v], hT[:, v % 2], bT[:], start=False, stop=True).then_inc(y_psum, 1)


_INS = ['L0_attn_x', 'L0_attn_wq', 'L0_attn_wk', 'L0_attn_wv', 'L0_attn_wo', 'L0_ffn_W_base', 'L0_ffn_b_base',
        'L0_ffn_W_router', 'L0_ffn_A_stack', 'L0_ffn_B_stack']


def _shape_constants():
    inv = 1.0 / THETA ** (np.arange(0, HD, 2)[:HD // 2].astype(np.float32) / HD)
    angle = np.outer(np.arange(S), inv).astype(np.float32)
    pair = (np.arange(P) % HD) // 2
    sign = np.where(np.arange(P) % 2 == 0, -1.0, 1.0).astype(np.float32)
    cos_t = np.ascontiguousarray(np.cos(angle).T[pair]).astype(np.float32)
    sin_t = np.ascontiguousarray(np.sin(angle).T[pair] * sign[:, None]).astype(np.float32)
    consts = np.zeros((P, 3 * P + E), np.float32)
    consts[:, 0:P] = np.eye(P)
    row, col = np.arange(P)[:, None], np.arange(P)[None, :]
    consts[:, P:2 * P] = np.where(col > row, MASKED, 0.0)
    consts[:, 2 * P:3 * P] = np.where(row > col, MASKED, 0.0)
    consts[:, 3 * P:] = np.arange(E)
    return {"cos_t": cos_t, "sin_t": sin_t, "consts": consts}


def kernel(**inputs):
    import concourse.bacc as bacc
    from concourse.bass_utils import run_bass_kernel_spmd

    nc = bacc.Bacc("TRN2", target_bir_lowering=False, num_devices=1)
    arrays = {f"in_{name}": np.ascontiguousarray(inputs[name]) for name in _INS}
    arrays.update(_shape_constants())
    args = [nc.dram_tensor(n, a.shape, mybir.dt.from_np(a.dtype), kind="ExternalInput").ap() for n, a in arrays.items()]
    args.append(nc.dram_tensor("out", (B, S, D), F32, kind="ExternalOutput").ap())
    preln_block(nc, *args)
    r = run_bass_kernel_spmd(nc, [arrays], core_ids=[0])
    return r.results[0]["out"]
```

```python
from contextlib import ExitStack

import numpy as np

import concourse.bass as bass
from concourse import mybir

F32 = mybir.dt.float32
F32R = mybir.dt.float32r
BF16 = mybir.dt.bfloat16
U32 = mybir.dt.uint32
ACT = mybir.ActivationFunctionType
ALU = mybir.AluOpType
AX = mybir.AxisListType

P = 128
B, S, D = 2, 1024, 512
H, HD = 32, 16
E, R = 8, 16
ER = E * R
KT = D // P
CHUNK = 512
CHUNKS = S // CHUNK
TPC = CHUNK // P
NCH = B * CHUNKS
QH = 4
NG = H // QH
ROUNDS = B * NG
GW = QH * HD
TT = S // P
PARTS = 3
SLOTS = 6
KROWS = SLOTS * HD
MROWS = KROWS + 2
THETA = 10000.0
EPS = 1e-5
SCALE = float(HD) ** -0.5
LORA_SCALE = 32.0 / R
MASKED = -1e30
RING = 3
FLIGHT = 2
PC = 4
TILES = B * TT
K_WEIGHTS, V_WEIGHTS = 0, 1
WEIGHT_TURNS = KT + 3
STAGED = 16 * (4 + KT)


def max_tasks():
    tasks = []
    for i in [*range(TPC, TT), *range(TPC)]:
        width = (i + 1) * P
        for part, w in enumerate([min(width, CHUNK)] + ([width - CHUNK] if width > CHUNK else [])):
            per = min(QH, CHUNK // w)
            per = 1 if per == 3 else per
            for h in range(0, QH, per):
                tasks.append((i, part, h, per, w))
    return tasks


def preln_block(nc, x, wq, wk, wv, wo, w_base, b_base, w_router, a_stack, b_stack, cos_t, sin_t, consts, out):
    tasks = max_tasks()
    NT = len(tasks)
    units = [(1, j) for j in range(TT)] + [(0, j) for j in range(TPC)]
    NU = len(units)
    assert NU % RING == 0 and NT % 2 == 0 and ROUNDS % RING == 1
    masked_units = [u for u, (c, j) in enumerate(units) if j >= c * TPC]
    MASKINGS = 2 * len(masked_units)
    last_of = {1: TT - 1, 0: TPC - 1}
    width = [CHUNK - max(0, j - c * TPC) * P for c, j in units]
    pieces_of_work = [(u, k) for u in range(1, NU) for k in range(3)]
    spans = [width[u] if k < 2 else width[u - 1] for u, k in pieces_of_work]
    LATE = sum(t[0] >= TPC for t in tasks)
    FIRST = 3
    extras, given = {"begin": [*range(FIRST)]}, FIRST
    for k, piece in enumerate(pieces_of_work):
        upto = max(given, NT * sum(spans[:k + 1]) // sum(spans))
        here = []
        for f in range(given, upto):
            here.append(f)
            if f == LATE + 1:
                here.append("M1")
        if piece == (3, 2):
            here.append("R")
        given = upto
        extras[piece] = here
    extras["end"] = ["M0"]
    order = [e for here in extras.values() for e in here]
    turn_of = {e: k for k, e in enumerate(e for e in order if e != "R")}
    TURNS = len(turn_of)
    FIRST_TURNS = NT + 2
    BANKS = 3
    def plan(k):
        if k == 0:
            return [("QK", 0), ("QK", 1), ("moments", 0), ("QK", 2), ("QK", 3), ("normal", 0), ("QK", 4), ("QK", 5), ("QK", 6), ("V", 0),
                    ("QK", 7), ("V", 1), ("T", 0), ("T", 1), ("V", 2), ("T", 2), ("T", 3), ("V", 3)]
        if k == NCH - 1:
            return [("QK", 0), ("QK", 1), ("V", 0), ("QK", 2), ("QK", 3), ("V", 1), ("QK", 4), ("QK", 5), ("QK", 6), ("QK", 7)]
        return [("QK", 0), ("QK", 1), ("V", 0), ("moments", 0), ("QK", 2), ("QK", 3), ("normal", 0), ("V", 1), ("QK", 4), ("QK", 5), ("T", 0), ("T", 1),
                ("V", 2), ("QK", 6), ("QK", 7), ("T", 2), ("T", 3), ("V", 3)]

    between = [("V", t) for t in range(TPC // 2, TPC)] + [("W", g) for g in range(2)]
    for f in range(NT):
        between.append(f)
        if f % 3 == 2 and f // 3 + 2 < WEIGHT_TURNS:
            between.append(("W", f // 3 + 2))
        if f == LATE + 1:
            between.append("M1")
    between.append("M0")
    ring_order = [e for e in between if not isinstance(e, tuple)]
    assert given == NT and RING % BANKS == 0

    with ExitStack() as ctx:
        def sb(name, shape, dt=F32):
            return ctx.enter_context(nc.sbuf_tensor(name, shape, dt))

        def sem(name):
            return ctx.enter_context(nc.semaphore(name))

        v_all = sb("v_all", [P, TT, ROUNDS * GW])
        cst = sb("cst", [P, 2 * P + E])
        ident_b = sb("ident_b", [P, P], BF16)
        mask_q = sb("mask_q", [P, P], BF16)
        wo_hl = sb("wo_hl", [P, 2, KT, D], F32R)
        wb_hl = sb("wb_hl", [P, 2, KT, D], F32R)
        ar_hl = sb("ar_hl", [P, 2, KT, ER + E], F32R)
        bt_hl = sb("bt_hl", [P, 2, D], F32R)
        bias = sb("bias", [P, D])
        small = sb("small", [P, 280])
        mxp = sb("mxp", [P, QH, TPC, 2])
        nm = sb("nm", [P, CHUNKS, QH, TPC])
        mrow = sb("mrow", [P, CHUNKS, 2, P], BF16)
        rc = sb("rc", [P, CHUNKS * QH * CHUNK // P])
        ident = cst[:, 0:P]
        iota = cst[:, 2 * P:2 * P + E]
        KB = 256

        def slicer(tensor):
            return lambda at, n: tensor[:, int(at * KB):int((at + n) * KB)]

        with ExitStack() as stage:
            def own(name, shape, dt=F32):
                return stage.enter_context(nc.sbuf_tensor(name, shape, dt))

            w_hl = own("w_hl", [P, 2, 3, KT, D], F32R)
            xT_hl = own("xT_hl", [P, 2, 2, KT, CHUNK], F32R)
            region = slicer(own("arena1", [P, 44 * KB]))
        xin = region(0, 8).rearrange("p (t d) -> p t d", t=TPC)
        cs = region(8, 8).rearrange("p (w n) -> p w n", w=2)
        qf, ro, sw, r1 = (region(16 + 4 * k, 4).rearrange("p (s n) -> p s n", s=2) for k in range(4))
        pc = region(32, 12).bitcast(BF16).rearrange("p (s a n) -> p s a n", s=PC, a=PARTS)
        w_raw = v_all[:].rearrange("p t n -> p (t n)")[:, 0:3 * KT * D].rearrange("p (w k n) -> p w k n", w=3, k=KT)
        wb_st = region(0, 8).rearrange("p (o n) -> p o n", o=KT)
        with ExitStack() as stage:
            region = slicer(stage.enter_context(nc.sbuf_tensor("arena2", [P, 124 * KB], F32)))
        qs = region(0, 24).bitcast(BF16).rearrange("p (s c h n) -> p s c h n", s=RING, c=CHUNKS, h=QH)
        ks = region(24, 24).bitcast(BF16).rearrange("p (s h n) -> p s h n", s=RING, h=QH)
        pr = region(48, 24).rearrange("p (s h n) -> p s h n", s=RING, h=QH)
        vs = region(72, 12).rearrange("p (s j h d) -> p s j h d", s=RING, j=TT, h=QH)
        ot = region(84, 4).rearrange("p (c n) -> p c n", c=2)
        rcb = region(88, 4)
        att = region(92, 32).rearrange("p (k n) -> p k n", k=KT * B)
        wo_st = region(48, 8).rearrange("p (k n) -> p k n", k=KT)
        a_st = region(56, 2)
        b_st = region(58, 2).rearrange("p (o e r) -> p o e r", o=KT, e=E)
        r_st = region(60, 2)[0:E]
        WEIGHT_SLOTS = 6
        w_copies = region(96, 12).rearrange("p (s n) -> p s n", s=WEIGHT_SLOTS)

        with ExitStack() as stage:
            stage.enter_context(nc.sbuf_tensor("last_queries", [P, 8 * KB], F32))
            at_hl = stage.enter_context(nc.sbuf_tensor("at_hl", [P, FLIGHT, 2, KT, P], F32R))
            xnT_hl = stage.enter_context(nc.sbuf_tensor("xnT_hl", [P, FLIGHT, 2, KT, P], F32R))
            stage.enter_context(nc.sbuf_tensor("last_keys", [P, 8 * KB], F32))
            hT_hl = stage.enter_context(nc.sbuf_tensor("hT_hl", [P, FLIGHT, 2, P], F32R))
            region = slicer(stage.enter_context(nc.sbuf_tensor("arena3", [P, 19 * KB], F32)))
        x1, x1b, xn, y3 = (region(4 * k, 4).rearrange("p (u n) -> p u n", u=FLIGHT) for k in range(4))
        h3 = region(16, 1).rearrange("p (u n) -> p u n", u=FLIGHT)
        low_rank = region(17, 2).rearrange("p (u n) -> p u n", u=FLIGHT)[:, :, 0:ER + E]
        xrf = v_all[:].rearrange("p j n -> p (j n)")

        ps = ctx.enter_context(nc.psum_tensor("ps", [P, 8, 512], F32))
        outs = nc.dram_tensor("outs", [ROUNDS, QH, 2 * HD, S], F32).ap()
        recs = nc.dram_tensor("recs", [ROUNDS, QH, S], F32).ap()
        pieces = nc.dram_tensor("pieces", [2, PARTS, ROUNDS, QH, HD, S], BF16).ap()

        stats = small[:, 0:24].rearrange("p (t n) -> p t n", t=4)
        mv = small[:, 24:32].rearrange("p (t n) -> p t n", t=4)
        veps = small[:, 32:36]
        rstd = small[:, 36:40]
        mhalf = small[:, 40:44]
        top = small[:, 48:80].rearrange("p (u n) -> p u n", u=4)
        topi = small[:, 80:112].bitcast(U32).rearrange("p (u n) -> p u n", u=4)
        idxf = small[:, 112:120].rearrange("p (u n) -> p u n", u=4)
        gap = small[:, 120:124]
        ex = small[:, 124:128]
        den = small[:, 128:132]
        w0 = small[:, 132:136]
        w1 = small[:, 136:140]
        comb0 = small[:, 144:176].rearrange("p (u n) -> p u n", u=4)
        comb = small[:, 176:208].rearrange("p (u n) -> p u n", u=4)
        comb1 = small[:, 240:272].rearrange("p (u n) -> p u n", u=4)

        consts_loaded, staged_wb, staged = sem("consts_loaded"), sem("staged_wb"), sem("staged")
        weights_loaded = [sem(f"weights_loaded{w}") for w in range(3)]
        wh_ready, wl_ready, wl_ready_pool = sem("wh_ready"), sem("wl_ready"), sem("wl_ready_pool")
        xh_ready, wth_ready = sem("xh_ready"), sem("wth_ready")
        tables_loaded = [sem(f"tables_loaded{c}") for c in range(CHUNKS)]
        x_loaded = sem("x_loaded")
        consts_ready, half_ready = sem("consts_ready"), sem("half_ready")
        aggr_done, rstd_ready, xn_ready = sem("aggr_done"), sem("rstd_ready"), sem("xn_ready")
        carried = sem("carried")
        stats_done, eps_added = sem("stats_done"), sem("eps_added")
        m1_ready = sem("m1_ready")
        dve_step = sem("dve_step")
        tp_ready, xT_ready = sem("tp_ready"), sem("xT_ready")
        qk_ready, qf_ready = sem("qk_ready"), sem("qf_ready")
        v_ready, v_copied = sem("v_ready"), sem("v_copied")
        t1_ready, ro_ready, p1_ready, r1_ready, p2_ready, p3_ready = (
            sem(n) for n in ("t1_ready", "ro_ready", "p1_ready", "r1_ready", "p2_ready", "p3_ready"))
        stored = [sem(f"stored{s}") for s in range(PC)]
        wt_ready, wt_copied, wt_low, wo_low = (sem(n) for n in ("wt_ready", "wt_copied", "wt_low", "wo_low"))
        ones_set, vs_ready = sem("ones_set"), sem("vs_ready")
        stack_loaded = [sem(f"stack_loaded{s}") for s in range(RING)]
        rows_loaded = [sem(f"rows_loaded{c}") for c in range(CHUNKS)]
        bank_filled, bank_emptied = sem("bank_filled"), sem("bank_emptied")
        nm_ready = sem("nm_ready")
        k_scores, exp_done, masked, pv_done = sem("k_scores"), sem("exp_done"), sem("masked"), sem("pv_done")
        o_copied, ot_stored = sem("o_copied"), [sem(f"ot_stored{c}") for c in range(CHUNKS)]
        dens_loaded, rec_ready, rec_stored = sem("dens_loaded"), sem("rec_ready"), sem("rec_stored")
        att_loaded, rcb_loaded = ([sem(f"{n}_loaded{v}") for v in range(2)] for n in ("att", "rcb"))
        divided = sem("divided")
        xr_loaded, tiles_there = sem("xr_loaded"), sem("tiles_there")
        ath_ready, atl_ready, wo_ready = sem("ath_ready"), sem("atl_ready"), sem("wo_ready")
        x1_ready, aggr3, eps3, rstd3, xn3 = (sem(n) for n in ("x1_ready", "aggr3", "eps3", "rstd3", "xn3"))
        xnT_ready, xnh_ready, xnl_ready, ar_ready = (sem(n) for n in ("xnT_ready", "xnh_ready", "xnl_ready", "ar_ready"))
        x1b_ready, gap_ready, ex_ready, h_ready = (sem(n) for n in ("x1b_ready", "gap_ready", "ex_ready", "h_ready"))
        hT_ready, hh_ready, hl_ready = sem("hT_ready"), sem("hh_ready"), sem("hl_ready")
        y_psum, y_read = sem("y_psum"), sem("y_read")
        y_stored = [sem(f"y_stored{u}") for u in range(FLIGHT)]

        TP, QK = (0, 1), (2, 3, 4, 5)

        def v_bank(k, t):
            return 2 if k == NCH - 1 and t == TPC - 1 else (7, 6)[t % 2]

        KS_BANK, RING_BANK, O_BANK = 0, 4, 7
        BASE, WO_BANK, XT_BANK, HT_BANK, AR_BANK = 0, 4, 6, 2, (3, 7)

        MAXIMA_DONE = BANKS + FIRST_TURNS + (ROUNDS - 1) * TURNS
        PERIOD = 2 * RING
        LOOPED = (ROUNDS - 1 - RING) // PERIOD * PERIOD
        assert LOOPED == 2 * PERIOD

        def tile_of(n):
            return n % NG // 2 * B + n // NG

        def looped_tile(i, u):
            return i * (tile_of(PERIOD + u) - tile_of(u)) + tile_of(u)

        def turn(n, e):
            if isinstance(n, int) and n == -1:
                return ring_order.index(e)
            return n * TURNS + (FIRST_TURNS + turn_of[e])

        def ring_bank(n, s, e):
            if isinstance(n, int):
                return RING_BANK + turn(n, e) % BANKS
            return RING_BANK + (FIRST_TURNS + s * TURNS + turn_of[e]) % BANKS

        def all_steps(eng, step, after={}):
            for t in range(FLIGHT):
                step(t, t)
                if t in after:
                    after[t]()
            with eng.Fori(0, (TILES - 2 * FLIGHT) // FLIGHT) as i:
                for u in range(FLIGHT):
                    step(i * FLIGHT + FLIGHT + u, u)
            for t in range(TILES - FLIGHT, TILES + 2):
                step(t, t % FLIGHT)

        def has(t, ahead):
            return not isinstance(t, int) or 0 <= t + ahead < TILES

        def att_tile(t):
            return att.rearrange("p (k b) n -> p k (b n)", b=B)[:, :, bass.ds(t * P, P)]

        def weight_turn(g):
            bank = ps[:, TP[g % 2]]
            if g < KT:
                return wb_hl[:, :, g], bank
            if g == KT:
                return ar_hl[:, :, :, 0:ER], bank.rearrange("p (k n) -> p k n", k=KT)
            if g == KT + 1:
                return ar_hl[:, :, :, ER:ER + E], bank[:, 0:KT * E].rearrange("p (k n) -> p k n", k=KT)
            return bt_hl[:], bank

        def weight_copy(g):
            flat = w_copies[:, g % WEIGHT_SLOTS]
            if g == KT:
                return flat.rearrange("p (k n) -> p k n", k=KT)
            if g == KT + 1:
                return flat[:, 0:KT * E].rearrange("p (k n) -> p k n", k=KT)
            return flat

        def alone(eng):
            eng.sem_inc(carried, 1)

        block = ctx.enter_context(nc.Block())
        xrows = x.rearrange("b (c t p) d -> (b c) p t d", c=CHUNKS, p=P)

        @block.sync
        def _(sp):
            for done in (*stored, *y_stored):
                sp.sem_inc(done, 16)
            for done in ot_stored:
                sp.sem_inc(done, 16)
            sp.dma_start(xin, xrows[0]).then_inc(x_loaded, 16)
            sp.dma_start(cst[:], consts).then_inc(consts_loaded, 16)
            for w, src in enumerate((wq, wk, wv)):
                sp.dma_start(w_raw[:, w], src.rearrange("(k p) n -> p k n", p=P)).then_inc(weights_loaded[w], 16)
                if w == 1:
                    sp.dma_start(cs[:, 0, 0:CHUNK], cos_t[:, 0:CHUNK]).then_inc(tables_loaded[0], 16)
                    sp.dma_start(cs[:, 1, 0:CHUNK], sin_t[:, 0:CHUNK]).then_inc(tables_loaded[0], 16)
            sp.dma_start(cs[:, 0, CHUNK:S], cos_t[:, CHUNK:S]).then_inc(tables_loaded[1], 16)
            sp.dma_start(cs[:, 1, CHUNK:S], sin_t[:, CHUNK:S]).then_inc(tables_loaded[1], 16)

            def load_round(n, s):
                for qk, dst, use in ((0, qs, (0, 0, 0, 1, 1, 2)), (1, ks, (0, 1, 2, 0, 1, 0))):
                    for slot, part in enumerate(use):
                        src = pieces[qk, part].rearrange("n h d t -> d n h t")[:, bass.ds(n, 1)].rearrange("d n h t -> d (n h) t")
                        if qk == 0:
                            src = src.rearrange("d h (c t) -> d c h t", c=CHUNKS)
                        sp.dma_start(dst[HD * slot:HD * (slot + 1), s], src).then_inc(stack_loaded[s], 16)

            def next_x(k):
                if k <= NCH:
                    sp.wait_ge(tp_ready, TPC * k)
                if k < NCH:
                    sp.dma_start(xin, xrows[k]).then_inc(x_loaded, 16)
                elif k == NCH:
                    sp.dma_start(wb_st, w_base.rearrange("(o p) n -> p o n", p=P)).then_inc(staged_wb, 16)
                    sp.wait_ge(v_ready, TPC * (NCH - 1))
                    sp.dma_start(a_st, a_stack.rearrange("e r n -> (e r) n")).then_inc(staged, 16)
                    sp.dma_start(r_st, w_router).then_inc(staged, 16)
                    for o in range(KT):
                        sp.dma_start(b_st[:, o], b_stack[:, o * P:(o + 1) * P, :].rearrange("e p r -> p e r")).then_inc(staged, 16)
                    sp.dma_start(wo_st, wo.rearrange("(k p) n -> p k n", p=P)).then_inc(staged, 16)

            next_x(1)
            sp.dma_start(bias[:], b_base.partition_broadcast(P)).then_inc(staged, 16)
            for k in range(NCH):
                b, c = k // CHUNKS, k % CHUNKS
                for m in range(2 * KT):
                    t = 2 * KT * k + m
                    if k == NCH - 1 and m == KT:
                        sp.wait_ge(qk_ready, NCH * 2 * KT - KT)
                        load_round(0, 0)
                    sp.wait_ge(p3_ready, 2 + t + 1)
                    dst = pieces[m // KT].rearrange("a n h d t -> (n h d) a t")
                    row = b * NG * GW + (m % KT) * P
                    sp.dma_start(dst[row:row + P, :, c * CHUNK:(c + 1) * CHUNK], pc[:, t % PC]).then_inc(stored[t % PC], 16)
                next_x(k + 2)
            sp.wait_ge(qk_ready, NCH * 2 * KT)
            load_round(1, 1)

            def load_rows(n, s, c):
                sp.wait_ge(bank_emptied, BANKS + turn(n - 1, ("M0", "M1")[c]) + 1)
                for a in range(2):
                    sp.dma_start(qs[KROWS + a:KROWS + a + 1, s, c].rearrange("p h (i t) -> p (h i) t", t=P),
                                 mrow[0:QH * TPC, c, a, :]).then_inc(rows_loaded[c], 16)

            def store_outputs(n, cc):
                sp.wait_ge(o_copied, 2 * n + cc + 2)
                alone(sp)
                c = CHUNKS - 1 - cc
                dst = outs[bass.ds(n, 1), :, :, c * CHUNK:(c + 1) * CHUNK].rearrange("n h r q -> (n h r) q")
                sp.dma_start(dst, ot[:, cc]).then_inc(ot_stored[cc], 16)

            def load_outputs(n, tile, half):
                sp.wait_ge(divided, n + 1)
                alone(sp)
                for cc in range(CHUNKS):
                    sp.wait_ge(ot_stored[cc], 16 * (n + 2))
                alone(sp)
                src = outs[bass.ds(n, 1)]
                dst = att[half * GW:(half + 1) * GW, bass.ds(tile, 1)].rearrange("p o n -> p (o n)")
                sp.dma_start(dst, src[:, :, 0:HD].rearrange("n h d q -> (n h) d q")).then_inc(att_loaded[half], 16)
                sp.wait_ge(rec_ready, n + 1)
                alone(sp)
                sp.dma_start(rc[:], src[:, :, HD].rearrange("n h (x w) -> (n h) x w", x=P // QH)).then_inc(dens_loaded, 16)

            def spread_reciprocals(n, half):
                sp.wait_ge(rec_ready, n + 2)
                alone(sp)
                flat = recs[bass.ds(n, 1)].rearrange("n h q -> (n h) q")
                sp.dma_start(flat.rearrange("h (x w) -> h x w", x=P // QH), rc[:]).then_inc(rec_stored, 16)
                sp.wait_ge(rec_stored, 16 * (n + 1))
                alone(sp)
                src = flat.unsqueeze(1).broadcast_to([QH, HD, S])
                sp.dma_start(rcb[half * GW:(half + 1) * GW], src).then_inc(rcb_loaded[half], 16)

            def sp_round(n, u, tile, load=True):
                load_rows(n + 1, (u + 1) % RING, 1)
                store_outputs(n, 0)
                load_rows(n + 1, (u + 1) % RING, 0)
                store_outputs(n, 1)
                load_outputs(n, tile, u % 2)
                if load:
                    sp.wait_ge(pv_done, RING + NU * (n + 1))
                    load_round(n + RING, u % RING)
                spread_reciprocals(n, u % 2)

            for s in range(PC):
                sp.wait_ge(stored[s], 16 * (1 + NCH * 2 * KT // PC))
            sp.wait_ge(v_copied, 2 + TPC * NCH)
            for n in range(2, RING):
                load_round(n, n)
            for c in (1, 0):
                load_rows(0, 0, c)
            with sp.Fori(0, LOOPED // PERIOD) as i:
                for u in range(PERIOD):
                    sp_round(i * PERIOD + u, u, looped_tile(i, u))
            for n in range(LOOPED, ROUNDS - 1):
                sp_round(n, n % PERIOD, tile_of(n), n + RING < ROUNDS)
                if n == ROUNDS - RING:
                    sp.wait_ge(vs_ready, ROUNDS)
                    sp.dma_start(xrf.rearrange("p (t d) -> p t d", d=D), x.rearrange("b (j p) d -> p (b j) d", p=P)).then_inc(
                        xr_loaded, 16)
            for cc in range(CHUNKS):
                store_outputs(ROUNDS - 1, cc)
            load_outputs(ROUNDS - 1, tile_of(ROUNDS - 1), (ROUNDS - 1) % 2)
            spread_reciprocals(ROUNDS - 1, (ROUNDS - 1) % 2)

            rows_out = out.rearrange("b (j p) d -> p (b j) d", p=P)
            with sp.Fori(0, TILES // FLIGHT) as i:
                for u in range(FLIGHT):
                    t = i * FLIGHT + u
                    sp.wait_ge(y_read, FLIGHT + t + 1)
                    alone(sp)
                    sp.dma_start(rows_out[:, bass.ds(t, 1)].rearrange("p o d -> p (o d)"), y3[:, u]).then_inc(y_stored[u], 16)
            for done in y_stored:
                sp.wait_ge(done, 16 + 16 * TILES // FLIGHT)

        @block.gpsimd
        def _(pool):
            nc.gpsimd.memset(mhalf, -0.5).then_inc(half_ready, 1)
            pool.sem_inc(p3_ready, 2)
            nc.gpsimd.memset(rc[:], 1.0).then_inc(dens_loaded, 16)
            pool.sem_inc(divided, 2)
            pool.sem_inc(x1b_ready, FLIGHT)
            pool.wait_ge(half_ready, 1)
            def rstd_of(k):
                pool.wait_ge(aggr_done, k + 1)
                nc.gpsimd.tensor_scalar(veps, mv[:, :, 1], EPS, 1.0, ALU.add, ALU.mult).then_inc(eps_added, 1)
                pool.wait_ge(eps_added, k + 1)
                nc.gpsimd.tensor_tensor(rstd, veps, mhalf, ALU.pow).then_inc(rstd_ready, 1)

            rstd_of(0)
            for k in range(NCH):
                c = k % CHUNKS
                pool.wait_ge(tables_loaded[c], 32)
                for kind, m in plan(k) + [("QK", 2 * KT), ("QK", 2 * KT + 1)]:
                    if kind == "moments":
                        rstd_of(k + 1)
                    if kind != "QK":
                        continue
                    t = k * 2 * KT + m
                    if m < 2 * KT:
                        pool.wait_ge(qf_ready, t + 1)
                        pool.wait_ge(r1_ready, t + 1)
                        nc.gpsimd.tensor_tensor(ro[:, m % 2], qf[:, m % 2], cs[:, 0, c * CHUNK:(c + 1) * CHUNK],
                                                ALU.mult).then_inc(t1_ready, 1)
                    if m >= 2:
                        pool.wait_ge(p2_ready, t - 1)
                        v = (m - 2) % PC
                        nc.gpsimd.tensor_tensor(pc[:, v, 2], r1[:, m % 2], pc[:, v, 1], ALU.subtract).then_inc(p3_ready, 1)
                    if k == 0 and m == V_WEIGHTS:
                        pool.wait_ge(wh_ready, 3)
                        nc.gpsimd.tensor_tensor(w_hl[:, 1, 2], w_raw[:, 2], w_hl[:, 0, 2].bitcast(F32), ALU.subtract).then_inc(
                            wl_ready_pool, 1)

            pool.wait_ge(qk_ready, NCH * 2 * KT)
            pool.wait_ge(p3_ready, 2 + NCH * 2 * KT)
            nc.gpsimd.memset(ks[KROWS:MROWS, 0], 1.0).then_inc(ones_set, 1)
            pool.wait_ge(ones_set, 1)
            for g in range(WEIGHT_TURNS):
                pool.wait_ge(wt_copied, g + 1)
                dst, _ = weight_turn(g)
                nc.gpsimd.tensor_tensor(dst[:, 1], weight_copy(g), dst[:, 0].bitcast(F32), ALU.subtract).then_inc(wt_low, 1)
            pool.wait_ge(wt_low, WEIGHT_TURNS)
            pool.wait_ge(wth_ready, WEIGHT_TURNS + 1)
            nc.gpsimd.tensor_tensor(wo_hl[:, 1], wo_st, wo_hl[:, 0].bitcast(F32), ALU.subtract).then_inc(wo_low, 1)
            pool.wait_ge(wt_copied, KT)
            pool.wait_ge(v_copied, 2 + TPC * NCH)
            nc.gpsimd.memset(vs[:, :, :, :, HD:2 * HD], 1.0).then_inc(ones_set, 1)

            def gather_v(n, s):
                src = v_all[:, :, bass.ds(n * GW, GW)].rearrange("p j (h d) -> p j h d", h=QH)
                nc.gpsimd.tensor_copy(vs[:, s, :, :, 0:HD], src).then_inc(vs_ready, 1)

            def divide(n, tile, half):
                pool.wait_ge(att_loaded[half], (n - half) * 8 + 16)
                pool.wait_ge(rcb_loaded[half], (n - half) * 8 + 16)
                pool.wait_ge(divided, n + 2)
                rows = slice(half * GW, (half + 1) * GW)
                a = att[rows, bass.ds(tile, 1)].rearrange("p o n -> p (o n)")
                nc.gpsimd.tensor_tensor(a, a, rcb[rows], ALU.mult).then_inc(divided, 1)

            zero = pool.to_reg(0.0)

            def low_att(t, u):
                pool.wait_ge(ath_ready, t + 1)
                nc.gpsimd.tensor_tensor(at_hl[:, u, 1], att_tile(t), at_hl[:, u, 0].bitcast(F32), ALU.subtract).then_inc(
                    atl_ready, 1)

            def pool_round(n, v, tile=None, gather=True):
                if gather:
                    pool.wait_ge(pv_done, RING + NU * n)
                    gather_v(n + RING - 1, (v + RING - 1) % RING)
                if tile is not None:
                    pool.wait_ge(vs_ready, n + RING if gather else ROUNDS)
                    pool.wait_ge(masked, MASKINGS * n)
                    divide(n - 2, tile, v % 2)
                    pool.wait_ge(divided, 1 + n)
                if isinstance(n, int) and n == ROUNDS - 1:
                    pool.sem_inc(tiles_there, TILES - TT)
                    for t in range(FLIGHT):
                        low_att(t, t)
                for u in masked_units:
                    for hp in range(2):
                        pool.wait_ge(exp_done, 2 + 2 * NU * n + 2 * u + hp + 1)
                        alone(pool)
                        block_of = pr[:, u % RING, 2 * hp:2 * hp + 2, 0:P]
                        nc.gpsimd.affine_select(block_of, block_of, [[0, 2], [1, P]], ALU.is_ge, zero, base=0,
                                                channel_multiplier=-1).then_inc(masked, 1)

            for n in range(RING - 1):
                gather_v(n, n)
            pool.wait_ge(vs_ready, RING - 1)
            pool.wait_ge(v_copied, 2 + TPC * NCH)
            nc.gpsimd.memset(ks[KROWS:MROWS, 1:RING], 1.0).then_inc(ones_set, 1)
            pool.wait_ge(ones_set, 3)
            for n in range(2):
                pool_round(n, n)
            with pool.Fori(0, LOOPED // PERIOD) as i:
                for u in range(PERIOD):
                    pool_round(i * PERIOD + (u + 2), u + 2, looped_tile(i, u))
            for n in range(LOOPED + 2, ROUNDS):
                pool_round(n, n % PERIOD, tile_of(n - 2), n + RING - 1 < ROUNDS)

            def divide_late(n):
                pool.wait_ge(x1b_ready, FLIGHT + n - (ROUNDS - 2) + 1)
                divide(n, tile_of(n), n % 2)
                pool.wait_ge(divided, 2 + n + 1)
                if n == ROUNDS - 1:
                    pool.sem_inc(tiles_there, TT)

            def pool_step(t, u):
                if has(t, 1) and not (isinstance(t, int) and t == 0):
                    low_att(t + 1, (u + 1) % FLIGHT)
                if has(t, 0):
                    pool.wait_ge(aggr3, t + 1)
                    alone(pool)
                    nc.gpsimd.tensor_scalar(veps[:, u:u + 1], mv[:, u, 1:2], EPS, 1.0, ALU.add, ALU.mult).then_inc(eps3, 1)
                    pool.wait_ge(eps3, t + 1)
                    nc.gpsimd.tensor_tensor(rstd[:, u:u + 1], veps[:, u:u + 1], mhalf[:, 0:1], ALU.pow).then_inc(rstd3, 1)
                    pool.wait_ge(y_read, t + 1)
                    nc.gpsimd.tensor_tensor(x1b[:, u], x1[:, u], bias[:], ALU.add).then_inc(x1b_ready, 1)

            all_steps(pool, pool_step, {t: lambda n=ROUNDS - 2 + t: divide_late(n) for t in range(FLIGHT)})

        @block.scalar
        def _(act):
            act.sem_inc(v_copied, 2)

            def high_weights(w):
                act.wait_ge(weights_loaded[w], 16)
                nc.scalar.copy(w_hl[:, 0, w], w_raw[:, w]).then_inc(wh_ready, 1)

            def high_x(k, t):
                act.wait_ge(tp_ready, k * TPC + t + 1)
                nc.scalar.copy(xT_hl[:, k % 2, 0, :, t * P:(t + 1) * P],
                               ps[:, TP[t % 2]].rearrange("p (k n) -> p k n", k=KT)).then_inc(xh_ready, 1)

            def copy_v(k, t):
                act.wait_ge(v_ready, k * TPC + t + 1)
                nc.scalar.copy(v_all[:, k % CHUNKS * TPC + t, k // CHUNKS * D:(k // CHUNKS + 1) * D], ps[:, v_bank(k, t)]).then_inc(
                    v_copied, 1)

            high_weights(0)
            for t in range(TPC):
                high_x(0, t)
            for k in range(NCH):
                for kind, m in plan(k) + [("QK", 2 * KT), ("QK", 2 * KT + 1)]:
                    if kind == "V":
                        copy_v(k, m)
                    if kind == "T":
                        high_x(k + 1, m)
                    if kind != "QK":
                        continue
                    t = k * 2 * KT + m
                    if m < 2 * KT:
                        act.wait_ge(qk_ready, t + 1)
                        nc.scalar.copy(qf[:, m % 2], ps[:, QK[m % 4]]).then_inc(qf_ready, 1)
                    if 1 <= m <= 2 * KT:
                        v = (m - 1) % PC
                        act.wait_ge(ro_ready, t)
                        act.wait_ge(stored[v], 16 + 16 * (k * (2 * KT // PC) + (m - 1) // PC))
                        nc.scalar.copy(pc[:, v, 0], ro[:, (m - 1) % 2]).then_inc(p1_ready, 1)
                    if m >= 2:
                        act.wait_ge(r1_ready, t + 1)
                        nc.scalar.copy(pc[:, (m - 2) % PC, 1], r1[:, m % 2]).then_inc(p2_ready, 1)
                    if k == 0 and m in (K_WEIGHTS, V_WEIGHTS):
                        high_weights(1 if m == K_WEIGHTS else 2)

            for e in between:
                if e in range(NT) or e in ("M1", "M0"):
                    continue
                kind, g = e
                if kind == "V":
                    copy_v(NCH - 1, g)
                else:
                    act.wait_ge(wt_ready, g + 1)
                    dst, src = weight_turn(g)
                    nc.scalar.copy(dst[:, 0], src).then_inc(wth_ready, 1)
                    if g >= WEIGHT_SLOTS:
                        act.wait_ge(wt_low, g - WEIGHT_SLOTS + 1)
                    nc.scalar.copy(weight_copy(g), src).then_inc(wt_copied, 1)
            nc.scalar.copy(wo_hl[:, 0], wo_st).then_inc(wth_ready, 1)

            def exps(n, u, slot):
                c, j = units[u]
                w = CHUNK - max(0, j - c * TPC) * P
                for hp in range(2):
                    act.wait_ge(k_scores, 2 * NU * n + 2 * u + hp + 1)
                    if hp == 0:
                        act.wait_ge(pv_done, NU * n + u + 1)
                    nc.scalar.activation(pr[:, slot, 2 * hp:2 * hp + 2, 0:w], ps[:, KS_BANK + 2 * hp:KS_BANK + 2 * hp + 2, 0:w],
                                         ACT.Exp, scale=SCALE).then_inc(exp_done, 1)

            def copy_output(n, cc, done):
                act.wait_ge(pv_done, RING + NU * n + done)
                act.wait_ge(ot_stored[cc], 16 * (n + 1))
                nc.scalar.copy(ot[:, cc], ps[:, O_BANK]).then_inc(o_copied, 1)

            def act_round(n):
                for u in range(1, NU):
                    exps(n, u, u % RING)
                    if u == TT:
                        copy_output(n, 0, TT)
                    if u == 3 and isinstance(n, int) and n == ROUNDS - 1:
                        for t in range(FLIGHT):
                            high_att(t, t)
                if not (isinstance(n, int) and n == ROUNDS - 1):
                    exps(n + 1, 0, 0)
                copy_output(n, 1, NU)

            def high_att(t, u):
                act.wait_ge(tiles_there, t + 1)
                nc.scalar.copy(at_hl[:, u, 0], att_tile(t)).then_inc(ath_ready, 1)

            act.sem_inc(exp_done, 2)
            act.sem_inc(o_copied, 1)
            exps(0, 0, 0)
            with act.Fori(0, (ROUNDS - 1) // RING) as i:
                for u in range(RING):
                    act_round(i * RING + u)
            act_round(ROUNDS - 1)

            def act_step(t, u):
                w = (u + 1) % FLIGHT
                if has(t, 1) and not (isinstance(t, int) and t == 0):
                    act.wait_ge(wo_ready, t)
                    high_att(t + 1, w)
                if has(t, -2):
                    act.wait_ge(hT_ready, t - 1)
                    nc.scalar.copy(hT_hl[:, u, 0], ps[:, HT_BANK, 0:P]).then_inc(hh_ready, 1)
                if has(t, -1):
                    act.wait_ge(gap_ready, t)
                    nc.scalar.activation(ex[:, w:w + 1], gap[:, w:w + 1], ACT.Exp).then_inc(ex_ready, 1)
                if has(t, 0):
                    act.wait_ge(xnT_ready, t + 1)
                    nc.scalar.copy(xnT_hl[:, u, 0], ps[:, XT_BANK].rearrange("p (k n) -> p k n", k=KT)).then_inc(xnh_ready, 1)

            all_steps(act, act_step)

        @block.vector
        def _(dve):
            steps = [0]

            def link(ins, base):
                steps[0] += 1
                ins.then_inc(dve_step, 1)
                dve.wait_ge(dve_step, base + steps[0])

            dve.sem_inc(r1_ready, 2)
            swap = [l ^ 1 for l in range(32)]

            def moments_of(k):
                dve.wait_ge(x_loaded, 16 * (k + 1))
                for t in range(TPC):
                    nc.vector.bn_stats(stats[:, t], xin[:, t]).then_inc(stats_done, 1)
                for t in range(TPC):
                    dve.wait_ge(stats_done, k * TPC + t + 1)
                    last = nc.vector.bn_aggr(mv[:, t], stats[:, t])
                last.then_inc(aggr_done, 1)

            def normal_of(k):
                dve.wait_ge(rstd_ready, k + 1)
                for t in range(TPC):
                    nc.vector.tensor_scalar(xin[:, t], xin[:, t], mv[:, t, 0:1], rstd[:, t:t + 1],
                                            ALU.subtract, ALU.mult).then_inc(xn_ready, 1)

            def low_x(k, t):
                dve.wait_ge(xh_ready, k * TPC + t + 1)
                cols = slice(t * P, (t + 1) * P)
                nc.vector.tensor_tensor(xT_hl[:, k % 2, 1, :, cols], ps[:, TP[t % 2]].rearrange("p (k n) -> p k n", k=KT),
                                        xT_hl[:, k % 2, 0, :, cols].bitcast(F32), ALU.subtract).then_inc(xT_ready, 1)

            moments_of(0)
            dve.wait_ge(consts_loaded, 16)
            nc.vector.tensor_copy(ident_b[:], ident)
            nc.vector.tensor_copy(mask_q[:], cst[:, P:2 * P]).then_inc(consts_ready, 1)
            normal_of(0)

            def low_weights(w):
                dve.wait_ge(wh_ready, w + 1)
                nc.vector.tensor_tensor(w_hl[:, 1, w], w_raw[:, w], w_hl[:, 0, w].bitcast(F32), ALU.subtract).then_inc(wl_ready, 1)

            low_weights(0)
            for t in range(TPC):
                low_x(0, t)
            low_weights(1)
            for k in range(NCH):
                c = k % CHUNKS
                dve.wait_ge(tables_loaded[c], 32)
                for kind, m in plan(k) + [("QK", 2 * KT)]:
                    if kind == "moments":
                        moments_of(k + 1)
                    if kind == "normal":
                        normal_of(k + 1)
                    if kind == "T":
                        low_x(k + 1, m)
                    if kind != "QK":
                        continue
                    t = k * 2 * KT + m
                    s = m % 2
                    if m < 2 * KT:
                        dve.wait_ge(qf_ready, t + 1)
                        link(nc.vector.stream_shuffle(sw[:, s], qf[:, s], swap), 0)
                        link(nc.vector.tensor_tensor(sw[:, s], sw[:, s], cs[:, 1, c * CHUNK:(c + 1) * CHUNK], ALU.mult), 0)
                        dve.wait_ge(t1_ready, t + 1)
                        nc.vector.tensor_tensor(ro[:, s], ro[:, s], sw[:, s], ALU.add).then_inc(ro_ready, 1)
                    if m >= 1:
                        v = (m - 1) % 2
                        dve.wait_ge(p1_ready, t)
                        dve.wait_ge(p3_ready, t)
                        nc.vector.tensor_tensor(r1[:, v], ro[:, v], pc[:, (m - 1) % PC, 0], ALU.subtract).then_inc(r1_ready, 1)
            base2 = steps[0]
            steps[0] = 0

            dve.sem_inc(bank_emptied, BANKS)

            def maximum(n, s, e):
                i, part, h, per, w = tasks[e]
                dve.wait_ge(bank_filled, turn(n, e) + 1)
                src = ps[:, ring_bank(n, s, e), 0:per * w].rearrange("p (h n) -> p h n", h=per)
                if i < TPC:
                    nc.vector.tensor_reduce(nm[:, 0, h:h + per, i], src, AX.X, ALU.max, negate=True).then_inc(bank_emptied, 1)
                else:
                    nc.vector.tensor_reduce(mxp[:, h:h + per, i - TPC, part], src, AX.X, ALU.max).then_inc(bank_emptied, 1)
                    if e == LATE - 1:
                        dve.wait_ge(bank_emptied, BANKS + turn(n, e) + 1)
                        nc.vector.tensor_reduce(nm[:, 1], mxp[:], AX.X, ALU.max, negate=True).then_inc(nm_ready, 1)

            def split_rows(n, s, e, m):
                c = ("M0", "M1").index(e)
                dve.wait_ge(bank_filled, turn(n, e) + 1)
                if not (isinstance(m, int) and m == 0):
                    dve.wait_ge(rows_loaded[c], m * 32)
                rows = ps[0:QH * TPC, ring_bank(n, s, e), 0:P]
                nc.vector.tensor_copy(mrow[0:QH * TPC, c, 0], rows).then_inc(m1_ready, 1)
                dve.wait_ge(m1_ready, 2 * m + 2 - c)
                nc.vector.tensor_tensor(mrow[0:QH * TPC, c, 1], rows, mrow[0:QH * TPC, c, 0], ALU.subtract).then_inc(
                    bank_emptied, 1)

            def reciprocals(n):
                dve.wait_ge(dens_loaded, 16 * (n + 2))
                alone(dve)
                nc.vector.reciprocal(rc[:], rc[:]).then_inc(rec_ready, 1)

            for e in between:
                if e in ("M1", "M0"):
                    split_rows(-1, -1, e, 0)
                elif e in range(NT):
                    maximum(-1, -1, e)
            with dve.Fori(0, (ROUNDS - 1) // RING) as i:
                for u in range(RING):
                    n = i * RING + u
                    for e in order:
                        if e in ("M1", "M0"):
                            split_rows(n, u, e, n + 1)
                        elif e == "R":
                            reciprocals(n - 1)
                        else:
                            maximum(n, u, e)

            dve.sem_inc(x1_ready, FLIGHT)
            dve.sem_inc(h_ready, FLIGHT)
            dve.sem_inc(y_read, FLIGHT)
            reciprocals(ROUNDS - 2)
            dve.wait_ge(xr_loaded, 16)
            dve.wait_ge(staged, STAGED)

            def moments(t, u, base):
                dve.wait_ge(x1b_ready, t + 1)
                dve.wait_ge(wo_ready, t + 1)
                nc.vector.tensor_tensor(x1[:, u], ps[:, WO_BANK + u], residual(t), ALU.add).then_inc(x1_ready, 1)
                dve.wait_ge(x1_ready, FLIGHT + t + 1)
                link(nc.vector.bn_stats(stats[:, u], x1[:, u]), base)
                alone(dve)
                nc.vector.bn_aggr(mv[:, u], stats[:, u]).then_inc(aggr3, 1)

            def residual(t):
                return xrf[:, t * D:(t + 1) * D] if isinstance(t, int) else xrf[:, bass.ds(t * D, D)]

            def top_two(t, u, base):
                dve.wait_ge(ar_ready, t + 1)
                both = ps[:, AR_BANK[u], 0:2 * (ER + E)].rearrange("p (a n) -> p n a", a=2)
                link(nc.vector.tensor_reduce(low_rank[:, u], both, AX.X, ALU.add), base)
                alone(dve)
                link(nc.vector.max(top[:, u], low_rank[:, u, ER:ER + E]), base)
                nc.vector.tensor_tensor(gap[:, u:u + 1], top[:, u, 1:2], top[:, u, 0:1], ALU.subtract).then_inc(gap_ready, 1)
                link(nc.vector.max_index(topi[:, u], top[:, u], low_rank[:, u, ER:ER + E]), base)
                link(nc.vector.tensor_copy(idxf[:, u], topi[:, u, 0:2]), base)

            def weigh(t, u, base):
                dve.wait_ge(ex_ready, t + 1)
                link(nc.vector.tensor_scalar(den[:, u:u + 1], ex[:, u:u + 1], 1.0, 1.0 / LORA_SCALE, ALU.add, ALU.mult), base)
                link(nc.vector.reciprocal(w0[:, u:u + 1], den[:, u:u + 1]), base)
                link(nc.vector.tensor_tensor(w1[:, u:u + 1], w0[:, u:u + 1], ex[:, u:u + 1], ALU.mult), base)
                link(nc.vector.tensor_scalar(comb0[:, u], iota, idxf[:, u, 0:1], w0[:, u:u + 1], ALU.is_equal, ALU.mult), base)
                link(nc.vector.tensor_scalar(comb1[:, u], iota, idxf[:, u, 1:2], w1[:, u:u + 1], ALU.is_equal, ALU.mult), base)
                link(nc.vector.tensor_tensor(comb[:, u], comb0[:, u], comb1[:, u], ALU.add), base)
                nc.vector.tensor_tensor(h3[:, u].rearrange("p (e r) -> p e r", e=E),
                                        low_rank[:, u, 0:ER].rearrange("p (e r) -> p e r", e=E),
                                        comb[:, u].unsqueeze(2).broadcast_to([P, E, R]), ALU.mult).then_inc(h_ready, 1)

            LINKS = (1, 3 + 1, 6)

            def dve_step_of(t, u):
                w = (u + 1) % FLIGHT
                steps[0] = 0
                first = isinstance(t, int) and t == 0
                base = base2 if first else t * sum(LINKS) + (base2 + LINKS[0] - sum(LINKS))
                if has(t, 0):
                    moments(t, u, base)
                if isinstance(t, int) and t == 1:
                    reciprocals(ROUNDS - 1)
                if has(t, -2):
                    dve.wait_ge(hh_ready, t - 1)
                    nc.vector.tensor_tensor(hT_hl[:, u, 1], ps[:, HT_BANK, 0:P], hT_hl[:, u, 0].bitcast(F32), ALU.subtract).then_inc(
                        hl_ready, 1)
                if has(t, -1):
                    top_two(t - 1, w, base)
                if has(t, 0):
                    dve.wait_ge(rstd3, t + 1)
                    nc.vector.tensor_scalar(xn[:, u], x1[:, u], mv[:, u, 0:1], rstd[:, u:u + 1],
                                            ALU.subtract, ALU.mult).then_inc(xn3, 1)
                if has(t, -1):
                    weigh(t - 1, w, base)
                if has(t, -2):
                    dve.wait_ge(y_stored[u], stored_before(t, u))
                    dve.wait_ge(x1b_ready, FLIGHT + t - 1)
                    dve.wait_ge(y_psum, t - 1)
                    nc.vector.tensor_tensor(y3[:, u], ps[:, BASE + u], x1b[:, u], ALU.add).then_inc(y_read, 1)
                if has(t, 0):
                    dve.wait_ge(xnh_ready, t + 1)
                    nc.vector.tensor_tensor(xnT_hl[:, u, 1], ps[:, XT_BANK].rearrange("p (k n) -> p k n", k=KT),
                                            xnT_hl[:, u, 0].bitcast(F32), ALU.subtract).then_inc(xnl_ready, 1)

            def stored_before(t, u):
                return (t - u) * (16 // FLIGHT)

            all_steps(dve, dve_step_of)

        @block.tensor
        def _(pe):
            mm, tr = nc.tensor.matmul, nc.tensor.transpose
            pe.wait_ge(consts_loaded, 16)

            def three_products(out_ap, stationary, moving, first, last_of_group):
                for p, (a, b) in enumerate(((0, 0), (0, 1), (1, 0))):
                    done = mm(out_ap, stationary(a), moving(b), start=first and p == 0, stop=last_of_group and p == 2)
                return done

            def transpose_x(k, t):
                pe.wait_ge(xn_ready, k * TPC + t + 1)
                if k * TPC + t >= 2:
                    pe.wait_ge(xT_ready, k * TPC + t - 1)
                for kt in range(KT):
                    last = tr(ps[:, TP[t % 2], kt * P:(kt + 1) * P], xin[:, t, kt * P:(kt + 1) * P], ident)
                last.then_inc(tp_ready, 1)

            def project_v(k, t):
                pe.wait_ge(v_copied, k * TPC + t + 1)
                if v_bank(k, t) in QK:
                    pe.wait_ge(qf_ready, k * 2 * KT + KT + 1)
                for kt in range(KT):
                    last = three_products(ps[:, v_bank(k, t)], lambda a: xT_hl[:, k % 2, a, kt, t * P:(t + 1) * P],
                                          lambda a: w_hl[:, a, 2, kt], kt == 0, kt == KT - 1)
                last.then_inc(v_ready, 1)

            for t in range(TPC):
                transpose_x(0, t)
            for k in range(NCH):
                pe.wait_ge(xT_ready, k * TPC + TPC)
                for kind, m in plan(k):
                    if kind == "V":
                        if (k, m) == (0, 0):
                            pe.wait_ge(wl_ready_pool, 1)
                        project_v(k, m)
                    if kind == "T":
                        transpose_x(k + 1, m)
                    if kind != "QK":
                        continue
                    if k == 0 and m == 0:
                        pe.wait_ge(wl_ready, 1)
                    if k == 0 and m == KT:
                        pe.wait_ge(wl_ready, 2)
                    if k > 0 or m >= 4:
                        pe.wait_ge(qf_ready, k * 2 * KT + m - 3)
                    for kt in range(KT):
                        last = three_products(ps[:, QK[m % 4]],
                                              lambda a: w_hl[:, a, m // KT, kt, (m % KT) * P:(m % KT + 1) * P],
                                              lambda a: xT_hl[:, k % 2, a, kt], kt == 0, kt == KT - 1)
                    last.then_inc(qk_ready, 1)

            def transpose_weights(g):
                if g == 0:
                    pe.wait_ge(staged_wb, 16)
                if g == KT:
                    pe.wait_ge(staged, STAGED)
                if g >= 2:
                    pe.wait_ge(wt_copied, g - 1)
                bank = ps[:, TP[g % 2]]
                for o in range(KT):
                    if g < KT:
                        last = tr(bank[:, o * P:(o + 1) * P], wb_st[:, o, g * P:(g + 1) * P], ident)
                    elif g == KT:
                        last = tr(bank[:, o * P:(o + 1) * P], a_st[:, o * P:(o + 1) * P], ident)
                    elif g == KT + 1:
                        last = tr(bank[:, o * E:(o + 1) * E], r_st[:, o * P:(o + 1) * P], cst[0:E, 0:E])
                    else:
                        last = tr(bank[:, o * P:(o + 1) * P], b_st[:, o].rearrange("p e r -> p (e r)"), ident)
                last.then_inc(wt_ready, 1)

            pe.wait_ge(consts_ready, 1)

            def extra(n, s, e):
                bank = ring_bank(n, s, e)
                pe.wait_ge(bank_emptied, turn(n, e) + 1)
                if e in ("M1", "M0"):
                    c = ("M0", "M1").index(e)
                    if c == 1:
                        pe.wait_ge(nm_ready, n + 2)
                    else:
                        pe.wait_ge(bank_emptied, BANKS + turn(n, NT - 1) + 1)
                    last = tr(ps[0:QH * TPC, bank, 0:P], nm[:, c].rearrange("p h i -> p (h i)"), ident)
                else:
                    i, part, h0, per, w = tasks[e]
                    v = (s + 1) % RING
                    diagonal = part * CHUNK + w == (i + 1) * P
                    for h in range(per):
                        o = ps[:, bank, h * w:(h + 1) * w]
                        last = mm(o, qs[0:KROWS, v, i // TPC, h0 + h, i % TPC * P:(i % TPC + 1) * P],
                                  ks[0:KROWS, v, h0 + h, part * CHUNK:part * CHUNK + w], start=True, stop=not diagonal)
                        if diagonal:
                            last = mm(o[:, w - P:w], ident_b[:], mask_q[:], start=False, stop=True)
                last.then_inc(bank_filled, 1)

            def times_v(n, s, u):
                c, j = units[u]
                q0 = max(0, j - c * TPC) * P
                pe.wait_ge(exp_done, 2 + 2 * NU * n + 2 * u + 2)
                if u in masked_units:
                    pe.wait_ge(masked, MASKINGS * n + 2 * masked_units.index(u) + 2)
                if u == 0:
                    pe.wait_ge(vs_ready, n + 1)
                if j == 0:
                    pe.wait_ge(o_copied, 2 * n + (u > 0) + 1)
                for h in range(QH):
                    last = mm(ps[2 * HD * h:2 * HD * (h + 1), O_BANK, q0:CHUNK], vs[:, s, j, h], pr[:, u % RING, h, 0:CHUNK - q0],
                              start=j == 0, stop=j == last_of[c])
                last.then_inc(pv_done, 1)

            def key_scores(n, s, u, hp):
                c, j = units[u]
                q0 = CHUNK - width[u]
                pe.wait_ge(exp_done, 2 * NU * n + 2 * u + hp + 1)
                for h in (2 * hp, 2 * hp + 1):
                    last = mm(ps[:, KS_BANK + h, 0:width[u]], ks[0:MROWS, s, h, j * P:(j + 1) * P], qs[0:MROWS, s, c, h, q0:CHUNK],
                              start=True, stop=True)
                last.then_inc(k_scores, 1)

            def first_scores(n, s):
                pe.wait_ge(rows_loaded[1], 32 * n + 32)
                for hp in range(2):
                    key_scores(n, s, 0, hp)

            EARLY = [(u, k) for u in range(5, NU) for k in range(3)][0:4 * KT:2]

            def project(t, u, kts):
                if kts[0] == 0:
                    pe.wait_ge(atl_ready, t + 1)
                    pe.wait_ge(x1_ready, t + 1)
                for kt in kts:
                    last = three_products(ps[:, WO_BANK + u], lambda a: at_hl[:, u, a, kt], lambda a: wo_hl[:, a, kt],
                                          kt == 0, kt == KT - 1)
                if kts[-1] == KT - 1:
                    last.then_inc(wo_ready, 1)

            def pe_round(n, s, following=True):
                if following:
                    loads = 16 * 2 * SLOTS
                    pe.wait_ge(stack_loaded[(s + 1) % RING], (n - s) * (loads // RING) + loads * (1 + (s == RING - 1)))
                if following:
                    for e in extras["begin"]:
                        extra(n, s, e)
                for u in range(1, NU):
                    if u == TT:
                        pe.wait_ge(rows_loaded[0], 32 * n + 32)
                    for k in range(3):
                        if k < 2:
                            key_scores(n, s, u, k)
                        else:
                            times_v(n, s, u - 1)
                        for e in extras[u, k]:
                            if following and e != "R":
                                extra(n, s, e)
                        if not following and (u, k) in EARLY:
                            e = EARLY.index((u, k))
                            project(e // KT, e // KT, [e % KT])
                if following:
                    pe.wait_ge(ones_set, 3)
                    first_scores(n + 1, (s + 1) % RING)
                times_v(n, s, NU - 1)
                if following:
                    extra(n, s, "M0")

            pe.sem_inc(pv_done, RING)
            for e in between:
                if e in range(NT) or e in ("M1", "M0"):
                    if e == 0:
                        pe.wait_ge(stack_loaded[0], 16 * 2 * SLOTS)
                        pe.wait_ge(qf_ready, NCH * 2 * KT)
                        pe.wait_ge(v_copied, NCH * TPC)
                    extra(-1, -1, e)
                elif e[0] == "V":
                    project_v(NCH - 1, e[1])
                else:
                    transpose_weights(e[1])
            pe.wait_ge(ones_set, 1)
            pe.wait_ge(wo_low, 1)
            pe.wait_ge(wt_copied, WEIGHT_TURNS)
            pe.wait_ge(v_copied, 2 + NCH * TPC)
            first_scores(0, 0)
            with pe.Fori(0, (ROUNDS - 1) // RING) as i:
                for u in range(RING):
                    pe_round(i * RING + u, u)
            pe.wait_ge(bank_emptied, MAXIMA_DONE)
            pe_round(ROUNDS - 1, 0, False)

            def pe_step(t, u):
                w = (u + 1) % FLIGHT
                if isinstance(t, int) and t == 1:
                    pe.wait_ge(o_copied, 1 + 2 * ROUNDS)
                if has(t, 0) and not (isinstance(t, int) and t < FLIGHT):
                    project(t, u, range(KT))
                if has(t, -2):
                    pe.wait_ge(h_ready, FLIGHT + t - 1)
                    tr(ps[:, HT_BANK, 0:P], h3[:, u], ident).then_inc(hT_ready, 1)
                if has(t, -1):
                    pe.wait_ge(xnl_ready, t)
                    pe.wait_ge(h_ready, t)
                    sums = ps[:, AR_BANK[w], 0:2 * (ER + E)].rearrange("p (a n) -> p a n", a=2)
                    for kt in range(KT):
                        if kt > 0:
                            mm(sums[:, 0], xnT_hl[:, w, 1, kt], ar_hl[:, 0, kt], start=False, stop=False)
                        last = mm(sums, xnT_hl[:, w, 0, kt], ar_hl[:, :, kt], start=kt == 0, stop=kt == KT - 1)
                        if kt == 0:
                            mm(sums[:, 0], xnT_hl[:, w, 1, kt], ar_hl[:, 0, kt], start=False, stop=False)
                    last.then_inc(ar_ready, 1)
                    pe.wait_ge(y_read, t)
                    for kt in range(KT):
                        three_products(ps[:, BASE + w], lambda a: xnT_hl[:, w, a, kt], lambda a: wb_hl[:, a, kt],
                                       kt == 0, False)
                if has(t, -2):
                    pe.wait_ge(hl_ready, t - 1)
                    three_products(ps[:, BASE + u], lambda a: hT_hl[:, u, a], lambda a: bt_hl[:, a], False, True).then_inc(y_psum, 1)
                if has(t, 0):
                    pe.wait_ge(xn3, t + 1)
                    for kt in range(KT):
                        last = tr(ps[:, XT_BANK, kt * P:(kt + 1) * P], xn[:, u, kt * P:(kt + 1) * P], ident)
                    last.then_inc(xnT_ready, 1)

            all_steps(pe, pe_step)


_INS = ['L0_attn_x', 'L0_attn_wq', 'L0_attn_wk', 'L0_attn_wv', 'L0_attn_wo', 'L0_ffn_W_base', 'L0_ffn_b_base',
        'L0_ffn_W_router', 'L0_ffn_A_stack', 'L0_ffn_B_stack']


def _shape_constants():
    inv = 1.0 / THETA ** (np.arange(0, HD, 2)[:HD // 2].astype(np.float32) / HD)
    angle = np.outer(np.arange(S), inv).astype(np.float32)
    pair = (np.arange(P) % HD) // 2
    sign = np.where(np.arange(P) % 2 == 0, -1.0, 1.0).astype(np.float32)
    cos_t = np.ascontiguousarray(np.cos(angle).T[pair]).astype(np.float32)
    sin_t = np.ascontiguousarray(np.sin(angle).T[pair] * sign[:, None]).astype(np.float32)
    consts = np.zeros((P, 2 * P + E), np.float32)
    consts[:, 0:P] = np.eye(P)
    row, col = np.arange(P)[:, None], np.arange(P)[None, :]
    consts[:, P:2 * P] = np.where(col > row, MASKED, 0.0)
    consts[:, 2 * P:] = np.arange(E)
    return {"cos_t": cos_t, "sin_t": sin_t, "consts": consts}


def kernel(**inputs):
    import concourse.bacc as bacc
    from concourse.bass_utils import run_bass_kernel_spmd

    nc = bacc.Bacc("TRN2", target_bir_lowering=False, num_devices=1)
    arrays = {f"in_{name}": np.ascontiguousarray(inputs[name]) for name in _INS}
    arrays.update(_shape_constants())
    args = [nc.dram_tensor(n, a.shape, mybir.dt.from_np(a.dtype), kind="ExternalInput").ap() for n, a in arrays.items()]
    args.append(nc.dram_tensor("out", (B, S, D), F32, kind="ExternalOutput").ap())
    preln_block(nc, *args)
    r = run_bass_kernel_spmd(nc, [arrays], core_ids=[0])
    return r.results[0]["out"]
```
